# Optimizing a Trainium2 kernel written in Bass

```python
import numpy as np
import jax
import jax.numpy as jnp

def _softmax(x, axis=-1):
    return jax.nn.softmax(x, axis=axis)
def _gelu(x):
    return jax.nn.gelu(x, approximate=True)
def _silu(x):
    return jax.nn.silu(x)
def _sigmoid(x):
    return jax.nn.sigmoid(x)
def _layernorm(x, axis=-1, eps=1e-5):
    m = jnp.mean(x, axis=axis, keepdims=True)
    v = jnp.var(x, axis=axis, keepdims=True)
    return (x - m) / jnp.sqrt(v + eps)
def _scatter_add(tgt, idx, src, axis=0):
    return tgt.at[idx].add(src)
def _segment_sum(src, seg, n):
    return jax.ops.segment_sum(src, seg, n)

kernel_name = 'mk_adj_resnorm_d2_adj_256_c4acf1'

def setup_inputs(seed: int = 0):
    np.random.seed(seed)
    _w = jnp.asarray
    def _rec_inputs():
        import jax
        import jax.numpy as jnp
        _gk = jax.random.key(seed)
        x = 7.22e-05 + 1 * jax.random.normal(jax.random.fold_in(_gk, 1), (128, 128, 256), jnp.float32)
        _a = jax.random.bernoulli(jax.random.fold_in(_gk, 2), 0.03125, (128, 128, 128))
        _a = jnp.logical_or(_a, jnp.swapaxes(_a, -1, -2))
        _a = jnp.logical_or(_a, jnp.eye(128, dtype=bool))
        _af = _a.astype(jnp.float32)
        adj = _af
        return x, adj
    x, adj = _rec_inputs()
    def _L0_gnn_setup():
        import jax, jax.numpy as jnp
        import numpy as np
        from jax import lax
        DIM = 256
        EPS = 1e-05

        def _bn(h, g, b, m, v):
            scale = g / jnp.sqrt(v + EPS)
            return h * scale[None, :, None] + (b - m * scale)[None, :, None]

        def _conv1d(h, w, pad):
            return lax.conv_general_dilated(h, w, window_strides=(1,), padding=[(pad, pad)], dimension_numbers=('NCH', 'OIH', 'NCH'))
        key = jax.random.key(seed)
        ks = jax.random.split(key, 16)
        bs, n, d = (16, 2048, DIM)
        s = 0.05
        return {'x': jax.random.normal(ks[0], (bs, n, d), jnp.float32), 'mask': jnp.ones((bs, n, n), jnp.float32), 'w_se': jax.random.normal(ks[1], (3, d), jnp.float32) * s, 'b_se': jnp.zeros((3,), jnp.float32), 'conv1_w': jax.random.normal(ks[2], (d, d, 1), jnp.float32) * s, 'bn1_g': jnp.ones((d,), jnp.float32), 'bn1_b': jnp.zeros((d,), jnp.float32), 'bn1_m': jnp.zeros((d,), jnp.float32), 'bn1_v': jnp.ones((d,), jnp.float32), 'conv2_w': jax.random.normal(ks[3], (d, d, 17), jnp.float32) * s, 'bn2_g': jnp.ones((d,), jnp.float32), 'bn2_b': jnp.zeros((d,), jnp.float32), 'bn2_m': jnp.zeros((d,), jnp.float32), 'bn2_v': jnp.ones((d,), jnp.float32), 'w_msg': jax.random.normal(ks[4], (d, d), jnp.float32) * s, 'b_msg': jnp.zeros((d,), jnp.float32), 'w_ih': jax.random.normal(ks[5], (3 * d, 2 * d), jnp.float32) * s, 'b_ih': jnp.zeros((3 * d,), jnp.float32), 'w_hh': jax.random.normal(ks[6], (3 * d, d), jnp.float32) * s, 'b_hh': jnp.zeros((3 * d,), jnp.float32)}
    _L0_gnn_all = _L0_gnn_setup()
    _L0_gnn_in = {k: v for k, v in _L0_gnn_all.items() if k in ('w_se', 'b_se', 'conv1_w', 'bn1_g', 'bn1_b', 'bn1_m', 'bn1_v', 'conv2_w', 'bn2_g', 'bn2_b', 'bn2_m', 'bn2_v', 'w_msg', 'b_msg', 'w_ih', 'b_ih', 'w_hh', 'b_hh', )}
    del _L0_gnn_all

    def _L1_gnn_setup():
        import jax, jax.numpy as jnp
        import numpy as np
        key = jax.random.key(seed)
        k1, k2, k3, k4 = jax.random.split(key, 4)
        B, N, F_in, F_out = (8, 2048, 256, 256)
        x = jax.random.normal(k1, (B, N, F_in), dtype=jnp.float32)
        adj = jax.random.uniform(k2, (B, N, N), dtype=jnp.float32)
        stdv = 1.0 / np.sqrt(F_out)
        weight = jax.random.uniform(k3, (F_in, F_out), dtype=jnp.float32, minval=-stdv, maxval=stdv)
        bias = jax.random.uniform(k4, (F_out,), dtype=jnp.float32, minval=-stdv, maxval=stdv)
        return {'x': x, 'adj': adj, 'weight': weight, 'bias': bias}
    _L1_gnn_all = _L1_gnn_setup()
    _L1_gnn_in = {k: v for k, v in _L1_gnn_all.items() if k in ('weight', 'bias', )}
    del _L1_gnn_all

    return {
        "x": x,
        "adj": adj,
        "L0_gnn_w_se": _L0_gnn_in["w_se"],
        "L0_gnn_b_se": _L0_gnn_in["b_se"],
        "L0_gnn_conv1_w": _L0_gnn_in["conv1_w"],
        "L0_gnn_bn1_g": _L0_gnn_in["bn1_g"],
        "L0_gnn_bn1_b": _L0_gnn_in["bn1_b"],
        "L0_gnn_bn1_m": _L0_gnn_in["bn1_m"],
        "L0_gnn_bn1_v": _L0_gnn_in["bn1_v"],
        "L0_gnn_conv2_w": _L0_gnn_in["conv2_w"],
        "L0_gnn_bn2_g": _L0_gnn_in["bn2_g"],
        "L0_gnn_bn2_b": _L0_gnn_in["bn2_b"],
        "L0_gnn_bn2_m": _L0_gnn_in["bn2_m"],
        "L0_gnn_bn2_v": _L0_gnn_in["bn2_v"],
        "L0_gnn_w_msg": _L0_gnn_in["w_msg"],
        "L0_gnn_b_msg": _L0_gnn_in["b_msg"],
        "L0_gnn_w_ih": _L0_gnn_in["w_ih"],
        "L0_gnn_b_ih": _L0_gnn_in["b_ih"],
        "L0_gnn_w_hh": _L0_gnn_in["w_hh"],
        "L0_gnn_b_hh": _L0_gnn_in["b_hh"],
        "L1_gnn_weight": _L1_gnn_in["weight"],
        "L1_gnn_bias": _L1_gnn_in["bias"],
    }

def reference(x, adj, L0_gnn_w_se, L0_gnn_b_se, L0_gnn_conv1_w, L0_gnn_bn1_g, L0_gnn_bn1_b, L0_gnn_bn1_m, L0_gnn_bn1_v, L0_gnn_conv2_w, L0_gnn_bn2_g, L0_gnn_bn2_b, L0_gnn_bn2_m, L0_gnn_bn2_v, L0_gnn_w_msg, L0_gnn_b_msg, L0_gnn_w_ih, L0_gnn_b_ih, L0_gnn_w_hh, L0_gnn_b_hh, L1_gnn_weight, L1_gnn_bias):
    import jax
    import jax.numpy as jnp
    def _L0_gnn_ref(x, mask, w_se, b_se, conv1_w, bn1_g, bn1_b, bn1_m, bn1_v, conv2_w, bn2_g, bn2_b, bn2_m, bn2_v, w_msg, b_msg, w_ih, b_ih, w_hh, b_hh):
        import jax, jax.numpy as jnp
        import numpy as np
        from jax import lax
        DIM = 256
        EPS = 1e-05

        def _bn(h, g, b, m, v):
            scale = g / jnp.sqrt(v + EPS)
            return h * scale[None, :, None] + (b - m * scale)[None, :, None]

        def _conv1d(h, w, pad):
            return lax.conv_general_dilated(h, w, window_strides=(1,), padding=[(pad, pad)], dimension_numbers=('NCH', 'OIH', 'NCH'))
        d = x.shape[-1]
        xc = jnp.transpose(x, (0, 2, 1))
        h = _bn(_conv1d(xc, conv1_w, 0), bn1_g, bn1_b, bn1_m, bn1_v)
        h = jax.nn.relu(h)
        h = _bn(_conv1d(h, conv2_w, 8), bn2_g, bn2_b, bn2_m, bn2_v)
        x_conv = jnp.transpose(jax.nn.relu(h + xc), (0, 2, 1))
        s = x @ w_se.T + b_se
        sq = jnp.sum(s * s, axis=-1)
        dist = sq[:, :, None] + sq[:, None, :] - 2.0 * jnp.einsum('bnd,bmd->bnm', s, s)
        A = jnp.exp(-dist) * mask
        msg = jax.nn.relu(x @ w_msg.T + b_msg)
        x_nmp = jnp.einsum('bnm,bmd->bnd', A, msg)
        x_in = jnp.concatenate([x_conv, x_nmp], axis=-1)
        gi = x_in @ w_ih.T + b_ih
        gh = x @ w_hh.T + b_hh
        gi_r, gi_z, gi_n = (gi[..., :d], gi[..., d:2 * d], gi[..., 2 * d:])
        gh_r, gh_z, gh_n = (gh[..., :d], gh[..., d:2 * d], gh[..., 2 * d:])
        r = jax.nn.sigmoid(gi_r + gh_r)
        z = jax.nn.sigmoid(gi_z + gh_z)
        nn_ = jnp.tanh(gi_n + r * gh_n)
        return (1.0 - z) * nn_ + z * x

    def _L1_gnn_ref(x, adj, weight, bias):
        import jax, jax.numpy as jnp
        import numpy as np
        support = jnp.einsum('bni,io->bno', x, weight)
        out = jnp.einsum('bnm,bmo->bno', adj, support)
        return out + bias

    x = _layernorm(x + _L0_gnn_ref(x, adj, L0_gnn_w_se, L0_gnn_b_se, L0_gnn_conv1_w, L0_gnn_bn1_g, L0_gnn_bn1_b, L0_gnn_bn1_m, L0_gnn_bn1_v, L0_gnn_conv2_w, L0_gnn_bn2_g, L0_gnn_bn2_b, L0_gnn_bn2_m, L0_gnn_bn2_v, L0_gnn_w_msg, L0_gnn_b_msg, L0_gnn_w_ih, L0_gnn_b_ih, L0_gnn_w_hh, L0_gnn_b_hh), axis=-1)
    x = _layernorm(x + _L1_gnn_ref(x, adj, L1_gnn_weight, L1_gnn_bias), axis=-1)
    return x


_drawn_inputs = setup_inputs


def setup_inputs(seed=0):
    import zlib

    import numpy as np

    out = dict(_drawn_inputs(seed))
    spreads = {'L0_gnn_b_se': (0.0, 0.8),
     'L0_gnn_bn1_g': (1.0, 0.2),
     'L0_gnn_bn1_b': (0.0, 0.1),
     'L0_gnn_bn1_m': (0.0, 0.1),
     'L0_gnn_bn1_v': (1.0, 0.537),
     'L0_gnn_bn2_g': (1.0, 0.2),
     'L0_gnn_bn2_b': (0.0, 0.428),
     'L0_gnn_bn2_m': (0.0, 0.316),
     'L0_gnn_bn2_v': (1.0, 0.2),
     'L0_gnn_b_msg': (0.0, 0.1),
     'L0_gnn_b_ih': (0.0, 0.1),
     'L0_gnn_b_hh': (0.0, 0.275)}
    factors = {'L1_gnn_bias': 3.423}
    for name, (base, spread) in spreads.items():
        noise = np.random.default_rng([zlib.crc32(name.encode()), seed]).standard_normal(out[name].shape)
        drawn = base * np.exp(spread * noise) if base else spread * noise
        out[name] = jnp.asarray(drawn.astype(out[name].dtype))
    for name, factor in factors.items():
        out[name] = (out[name] * factor).astype(out[name].dtype)
    return out
```

```python
from contextlib import ExitStack

import concourse.bass as bass
from concourse import mybir

F32 = mybir.dt.float32
F32R = mybir.dt.float32r
ALU = mybir.AluOpType
ACT = mybir.ActivationFunctionType

P = 128
KT = 2
D = KT * P
GB = 4
COLS = GB * P
GROUPS = 32
TAPS = 17
PAD = TAPS // 2
PADDED = P + 2 * PAD
EPS = 1e-5
SE = 3
SE_ROWS = 2 * 32 + SE


def wait(engine, semaphore, count):
    if not isinstance(count, int) or count > 0:
        engine.wait_ge(semaphore, count)


def rounded_parts(engine, chain, high, low, value):
    sem, n = chain
    engine.tensor_copy(high, value).then_inc(sem, 1)
    engine.wait_ge(sem, n + 1)
    engine.tensor_tensor(low, value, high.bitcast(F32), ALU.subtract).then_inc(sem, 1)
    return sem, n + 2


def conv_branch(nc, xT, conv1_wT, conv2_wT, bn, x_conv):
    with ExitStack() as ctx:
        def sb(name, shape, dt=F32):
            return ctx.enter_context(nc.sbuf_tensor(name, shape, dt))

        def sem(name):
            return ctx.enter_context(nc.semaphore(name))

        w1 = [sb(f"conv1_{part}", [P, KT, D], F32R) for part in ("high", "low")]
        w2 = [sb(f"conv2_{part}", [P, KT, TAPS, D], F32R) for part in ("high", "low")]
        w1_raw = sb("conv1_raw", [P, KT, D])
        w2_raw = sb("conv2_raw", [P, 2, TAPS * D])
        bn_raw = sb("bn_raw", [P, 8, KT])
        bn_tmp = sb("bn_tmp", [P, 4, KT])
        minus_half = sb("minus_half", [P, 2 * KT])
        scale = sb("bn_scale", [P, 2, KT])
        shift = sb("bn_shift", [P, 2, KT])
        x = [sb(f"cx_{i}", [P, KT, COLS]) for i in range(2)]
        xh = [sb(f"cxh_{i}", [P, KT, COLS], F32R) for i in range(2)]
        xl = [sb(f"cxl_{i}", [P, KT, COLS], F32R) for i in range(2)]
        h = [sb(f"h_{i}", [P, KT, GB, P]) for i in range(2)]
        hh = [sb(f"hh_{i}", [P, KT, GB, PADDED], F32R) for i in range(2)]
        hl = [sb(f"hl_{i}", [P, KT, GB, PADDED], F32R) for i in range(2)]
        z = [sb(f"z_{i}", [P, KT, COLS]) for i in range(2)]
        y = [sb(f"y_{i}", [P, KT, COLS]) for i in range(2)]
        p1 = ctx.enter_context(nc.psum_tensor("p1", [P, KT, COLS], F32))
        p2 = [ctx.enter_context(nc.psum_tensor(f"p2_{i}", [P, KT, COLS], F32)) for i in range(2)]

        s_small = sem("small_loaded")
        s_w2 = sem("conv2_loaded")
        s_w = sem("conv_parts")
        s_bn = sem("bn_chain")
        s_zero = sem("pads_zeroed")
        s_x = [sem(f"cx_loaded_{i}") for i in range(2)]
        s_xh = sem("cx_high")
        s_xl = sem("cx_low")
        s_c1 = sem("conv1_done")
        s_h = sem("h_ready")
        s_hh = sem("hh_ready")
        s_hl = sem("hl_ready")
        s_c2 = sem("conv2_done")
        s_z = sem("z_ready")
        s_y = sem("y_ready")
        s_st = [sem(f"x_conv_stored_{i}") for i in range(2)]
        block = ctx.enter_context(nc.Block())

        @block.sync
        def _(sp):
            sp.dma_start(w1_raw[:], conv1_wT).then_inc(s_small, 16)
            sp.dma_start(bn_raw[:], bn).then_inc(s_small, 16)

            def load(g, i, count):
                sp.dma_start(x[i][:], xT[g].rearrange("k p c -> p k c")).then_inc(s_x[i], 16)

            for g in range(2):
                load(g, g, 1)
            for k in range(KT):
                sp.dma_start(w2_raw[:, k, :], conv2_wT[k]).then_inc(s_w2, 16)
            with sp.Fori(0, GROUPS // 2 - 1) as t:
                for i in range(2):
                    sp.wait_ge(s_z, KT * (2 * t + i + 1))
                    load(2 * t + i + 2, i, None)

        @block.gpsimd
        def _(pool):
            last = None
            for i in range(2):
                for part in (hh[i], hl[i]):
                    for edge in (part[:, :, :, 0:PAD], part[:, :, :, PADDED - PAD:PADDED]):
                        pool.memset(edge.bitcast(F32), 0.0).then_inc(s_zero, 1)
            pool.memset(minus_half[:], -0.5).then_inc(s_bn, 1)
            pool.wait_ge(s_small, 32)
            v = bn_raw[:, 6:8, :]
            pool.tensor_scalar(bn_tmp[:, 0:2, :], v, EPS, None, ALU.add).then_inc(s_bn, 1)
            pool.wait_ge(s_bn, 2)
            pool.tensor_tensor(bn_tmp[:, 2:4, :], bn_tmp[:, 0:2, :],
                               minus_half[:].rearrange("p (a k) -> p a k", a=2), ALU.pow).then_inc(s_bn, 1)
            pool.wait_ge(s_bn, 3)
            pool.tensor_tensor(scale[:], bn_tmp[:, 2:4, :], bn_raw[:, 0:2, :], ALU.mult).then_inc(s_bn, 1)
            pool.wait_ge(s_bn, 4)
            pool.tensor_tensor(bn_tmp[:, 0:2, :], bn_raw[:, 4:6, :], scale[:], ALU.mult).then_inc(s_bn, 1)
            pool.wait_ge(s_bn, 5)
            pool.tensor_tensor(shift[:], bn_raw[:, 2:4, :], bn_tmp[:, 0:2, :], ALU.subtract).then_inc(s_bn, 1)

            def low_part(g, i):
                pool.wait_ge(s_xh, g + 1)
                if not (isinstance(g, int) and g < 2):
                    pool.wait_ge(s_c1, KT * (g - 1))
                pool.tensor_tensor(xl[i][:], x[i][:], xh[i][:].bitcast(F32), ALU.subtract).then_inc(s_xl, 1)

            for g in range(2):
                low_part(g, g)
            with pool.Fori(1, GROUPS // 2) as t:
                for i in range(2):
                    low_part(2 * t + i, i)

        @block.vector
        def _(dve):
            dve.wait_ge(s_small, 32)
            chain = rounded_parts(dve, (s_w, 0), w1[0][:], w1[1][:], w1_raw[:])
            for k in range(KT):
                dve.wait_ge(s_w2, 16 * KT if k == KT - 1 else 16 * KT)
                chain = rounded_parts(dve, chain, w2[0][:, k], w2[1][:, k],
                                      w2_raw[:, k, :].rearrange("p (t o) -> p t o", t=TAPS))

            def split_h(g, i):
                for k in range(KT):
                    dve.wait_ge(s_h, KT * g + k + 1)
                    if not (isinstance(g, int) and g < 2):
                        dve.wait_ge(s_c2, KT * (g - 1))
                    inner = slice(PAD, PAD + P)
                    dve.tensor_copy(hh[i][:, k, :, inner], h[i][:, k]).then_inc(s_hh, 1)
                    dve.wait_ge(s_hh, KT * g + k + 1)
                    dve.tensor_tensor(hl[i][:, k, :, inner], h[i][:, k],
                                      hh[i][:, k, :, inner].bitcast(F32), ALU.subtract).then_inc(s_hl, 1)

            def residual(g, i):
                for k in range(KT):
                    dve.wait_ge(s_c2, KT * g + k + 1)
                    if not (isinstance(g, int) and g < 2):
                        dve.wait_ge(s_y, KT * (g - 1))
                    dve.scalar_tensor_tensor(z[i][:, k, :], p2[i][:, k, :], scale[:, 1, k:k + 1],
                                             x[i][:, k, :], ALU.mult, ALU.add).then_inc(s_z, 1)

            dve.wait_ge(s_bn, 6)
            split_h(0, 0)
            for i in range(2):
                split_h(i + 1, 1 - i)
                residual(i, i)
            with dve.Fori(1, GROUPS // 2 - 1) as t:
                for i in range(2):
                    split_h(2 * t + i + 1, 1 - i)
                    residual(2 * t + i, i)
            split_h(GROUPS - 1, 1)
            residual(GROUPS - 2, 0)
            residual(GROUPS - 1, 1)

        @block.scalar
        def _(act):
            def bn1_relu(g, i):
                for k in range(KT):
                    act.wait_ge(s_c1, KT * g + k + 1)
                    if not (isinstance(g, int) and g < 2):
                        act.wait_ge(s_hl, KT * (g - 1))
                    act.activation(h[i][:, k].rearrange("p b n -> p (b n)"), p1[:, k, :], ACT.Relu,
                                   bias=shift[:, 0, k:k + 1], scale=scale[:, 0, k:k + 1]).then_inc(s_h, 1)

            def bn2_relu_at(t, i, first):
                g = 2 * t + i
                for k in range(KT):
                    act.wait_ge(s_z, KT * g + k + 1)
                    if not first:
                        act.wait_ge(s_st[i], 16 * t)
                    act.activation(y[i][:, k, :], z[i][:, k, :], ACT.Relu,
                                   bias=shift[:, 1, k:k + 1]).then_inc(s_y, 1)
                act.wait_ge(s_y, KT * (g + 1))
                act.dma_start(x_conv[g].rearrange("k p c -> p k c"), y[i][:]).then_inc(s_st[i], 16)

            def high_part(g, i, t):
                act.wait_ge(s_x[i], 16 * (t + 1))
                if not (isinstance(g, int) and g < 2):
                    act.wait_ge(s_c1, KT * (g - 1))
                act.activation(xh[i][:], x[i][:], ACT.Copy).then_inc(s_xh, 1)

            high_part(0, 0, 0)
            act.wait_ge(s_bn, 6)
            bn1_relu(0, 0)
            for i in range(2):
                high_part(i + 1, 1 - i, i)
                bn1_relu(i + 1, 1 - i)
                bn2_relu_at(0, i, True)
            with act.Fori(1, GROUPS // 2 - 1) as t:
                for i in range(2):
                    high_part(2 * t + i + 1, 1 - i, t + i)
                    bn1_relu(2 * t + i + 1, 1 - i)
                    bn2_relu_at(t, i, False)
            high_part(GROUPS - 1, 1, GROUPS // 2 - 1)
            bn1_relu(GROUPS - 1, 1)
            for i in range(2):
                bn2_relu_at(GROUPS // 2 - 1, i, False)
            for i in range(2):
                act.wait_ge(s_st[i], 16 * (GROUPS // 2))

        @block.tensor
        def _(pe):
            def conv1(g, i):
                pe.wait_ge(s_xl, g + 1)
                for o in range(KT):
                    if not (isinstance(g, int) and g < 1):
                        pe.wait_ge(s_h, KT * (g - 1) + o + 1)
                    n = 0
                    for wt, xt in ((w1[0], xh[i]), (w1[0], xl[i]), (w1[1], xh[i])):
                        for k in range(KT):
                            mm = nc.tensor.matmul(p1[:, o, :], wt[:, k, o * P:(o + 1) * P], xt[:, k, :],
                                                  start=n == 0, stop=n == 5)
                            n += 1
                    mm.then_inc(s_c1, 1)

            def conv2(g, i, o):
                if not (isinstance(g, int) and g < 2):
                    pe.wait_ge(s_z, KT * (g - 1))
                pe.wait_ge(s_hl, KT * (g + 1))
                n = 0
                for wt, ht in ((w2[0], hh[i]), (w2[0], hl[i]), (w2[1], hh[i])):
                    for k in range(KT):
                        for t in range(TAPS):
                            mm = nc.tensor.matmul(p2[i][:, o, :].rearrange("p (b n) -> p b n", b=GB),
                                                  wt[:, k, t, o * P:(o + 1) * P],
                                                  ht[:, k, :, t:t + P],
                                                  start=n == 0, stop=n == 6 * TAPS - 1)
                            n += 1
                mm.then_inc(s_c2, 1)

            def step(g, i, more=True):
                conv2(g, i, 0)
                if more:
                    conv1(g + 1, 1 - i)
                conv2(g, i, 1)

            pe.wait_ge(s_w, 2)
            conv1(0, 0)
            pe.wait_ge(s_zero, 8)
            pe.wait_ge(s_w, 2 + 2 * KT)
            for i in range(2):
                step(i, i)
            with pe.Fori(1, GROUPS // 2 - 1) as t:
                for i in range(2):
                    step(2 * t + i, i)
            step(GROUPS - 2, 0)
            step(GROUPS - 1, 1, more=False)

def gated_layer_and_graph_layer(nc, xT, adjT, x_conv, w_seT, w_msgT, w_ihT, w_hhT, w_l1, se_bias,
                                msg_bias, gate_bias, l1_bias, identity, out):
    with ExitStack() as ctx:
        def sb(name, shape, dt=F32):
            return ctx.enter_context(nc.sbuf_tensor(name, shape, dt))

        def sem(name):
            return ctx.enter_context(nc.semaphore(name))

        def bank(name):
            return ctx.enter_context(nc.psum_tensor(name, [P, COLS], F32))

        def pair(name, shape):
            return [sb(f"{name}_{part}", shape, F32R) for part in ("high", "low")]

        w_se = pair("w_se", [P, KT, SE_ROWS])
        w_msg = pair("w_msg", [P, KT, D])
        w_ih = pair("w_ih", [P, 2 * KT, 3 * D])
        w_hh = pair("w_hh", [P, KT, 3 * D])
        w_1 = pair("w_1", [P, KT, D])
        raw = sb("w_raw", [P, 2, 3 * D])
        ident = sb("ident", [P, P])
        bse = sb("se_bias_rows", [P, 1])
        bmsg_raw = sb("bmsg_raw", [P, D])
        bmsg = sb("bmsg", [2, D], F32R)
        bl1 = sb("bl1", [P, D])
        bg_raw = sb("bg_raw", [P, 8, KT])
        bg = sb("bg", [P, 4, KT])
        minus_half = sb("minus_half2", [P, GB])
        eps = sb("eps", [P, GB])
        carrier = sb("wait_carrier", [P, 1])

        x = [sb(f"x_{i}", [P, KT, COLS]) for i in range(2)]
        xp = [pair(f"x{i}", [P, KT, COLS]) for i in range(2)]
        xc = [sb(f"xc_{i}", [P, KT, COLS]) for i in range(2)]
        xcp = pair("xc", [P, KT, COLS])
        adj = sb("adj", [P, COLS])
        adj_o = sb("adj_o", [P, COLS])
        adjp = pair("adj", [P, COLS])
        se = sb("se", [P, COLS])
        left = sb("left", [P, COLS])
        right = sb("right", [P, COLS])
        ones = sb("ones", [P, COLS])
        e = sb("e", [P, COLS])
        a = sb("a", [P, COLS])
        ap = pair("a", [P, COLS])
        msg_sum = sb("msg_sum", [P, KT, COLS])
        msgp = pair("msg", [P, KT, COLS])
        nmpp = pair("nmp", [P, KT, COLS])
        r = sb("r", [P, KT, COLS])
        z = sb("zg", [P, KT, COLS])
        n_in = sb("n_in", [P, KT, COLS])
        n = sb("n", [P, KT, COLS])
        u = sb("u", [P, KT, COLS])
        stats = sb("stats", [P, 2, GB, 6])
        moments = sb("moments", [P, 2, GB, 2])
        rstd = sb("rstd", [P, 2, GB])
        x2 = sb("x2", [P, GB, D])
        x2b = [sb(f"x2b_{i}", [P, GB, D]) for i in range(2)]
        x2p = pair("x2", [P, KT, COLS])
        supp = pair("sup", [P, GB, D])
        y = sb("y2", [P, GB, D])
        res = sb("res", [P, GB, D])

        gate_banks = [bank(f"gate_{i}") for i in range(3)]
        work = [bank(f"work_{i}") for i in range(5)]

        s_load = sem("weights_loaded")
        s_vec = sem("vectors_loaded")
        s_wd = sem("weight_parts")
        s_init = sem("constants_ready")
        s_bg = sem("gate_bias_chain")
        s_x = [sem(f"x_loaded_{i}") for i in range(2)]
        s_xc = [sem(f"xc_loaded_{i}") for i in range(2)]
        s_adj = sem("adj_loaded")
        s_adjo = sem("adj_o_loaded")
        names = {}
        for name in ("x_high", "x_low", "xc_high", "xc_low", "se", "left", "right", "e", "a", "a_high",
                     "a_low", "adj_high", "adj_low", "msg_sum", "msg_high", "msg_low", "nmp_high", "nmp_low",
                     "r_tanh", "r_done", "z_tanh", "z_done", "rn", "n_in", "n_done", "diff", "zdiff", "nx",
                     "u_done", "stats", "moments", "var", "rstd", "x2", "x2b", "x2T_high", "x2T_low",
                     "sup_high", "sup_low", "y", "ystats", "ymoments", "yvar", "yrstd", "res",
                     "pe_se", "pe_msg", "pe_dist", "pe_nmp", "pe_r", "pe_hn", "pe_in", "pe_z",
                     "pe_uT", "pe_x2T", "pe_sup", "pe_out"):
            names[name] = sem("q_" + name)
        S = names
        s_out = sem("out_stored")
        block = ctx.enter_context(nc.Block())

        def steps(engine, step):
            def at(g, i):
                def has(k):
                    return 0 <= k < GROUPS
                step(g, i, g // 2, has(g), has(g + 1), has(g - 1), has(g - 2))

            for g in (-1, 0, 1):
                at(g, g % 2)
            with engine.Fori(1, GROUPS // 2 - 1) as t:
                for i in range(2):
                    step(2 * t + i, i, t, True, True, True, True)
            for g in range(GROUPS - 2, GROUPS + 2):
                at(g, g % 2)

        @block.sync
        def _(sp):
            weights = [(w_msgT, KT, D), (w_seT, KT, SE_ROWS), (w_l1, KT, D),
                       (w_ihT[0:KT * P], KT, 3 * D), (w_ihT[KT * P:], KT, 3 * D), (w_hhT, KT, 3 * D)]
            for dst, src in ((ident, identity), (bse, se_bias), (bmsg_raw, msg_bias), (bl1, l1_bias),
                             (bg_raw, gate_bias)):
                sp.dma_start(dst[:], src).then_inc(s_vec, 16)
            for j, (src, k, m) in enumerate(weights):
                if j:
                    sp.wait_ge(s_wd, 2 * j)
                sp.dma_start(raw[:, :, 0:m], src.rearrange("(k p) m -> p k m", p=P)).then_inc(s_load, 16)

            def step(g, i, t, now, ahead, behind, last):
                if ahead:
                    wait(sp, S["u_done"], KT * g)
                    sp.dma_start(x[1 - i][:], xT[g + 1].rearrange("k p c -> p k c")).then_inc(s_x[1 - i], 16)
                    wait(sp, S["xc_low"], g)
                    sp.dma_start(xc[1 - i][:], x_conv[g + 1].rearrange("k p c -> p k c")).then_inc(s_xc[1 - i], 16)
                    wait(sp, S["a"], g + 1)
                    sp.dma_start(adj[:], adjT[g + 1]).then_inc(s_adj, 16)
                if behind:
                    wait(sp, S["adj_low"], g - 1)
                    sp.dma_start(adj_o[:], adjT[g - 1]).then_inc(s_adjo, 16)
                if last:
                    sp.wait_ge(S["res"], GB * (g - 1))
                    sp.dma_start(out[bass.ts(g - 2, GB)].rearrange("b n d -> n b d"), res[:]).then_inc(s_out, 16)

            steps(sp, step)
            sp.wait_ge(s_out, 16 * GROUPS)

        @block.gpsimd
        def _(pool):
            pool.memset(ones[:], 1.0).then_inc(s_init, 1)
            pool.memset(left[:], 0.0).then_inc(s_init, 1)
            pool.memset(right[:], 0.0).then_inc(s_init, 1)
            pool.memset(minus_half[:], -0.5).then_inc(s_init, 1)
            pool.memset(eps[:], EPS).then_inc(s_init, 1)
            pool.wait_ge(s_init, 5)
            pool.memset(left[64:64 + SE, :], -1.0).then_inc(s_init, 1)
            pool.wait_ge(s_init, 6)
            pool.memset(right[32:32 + SE, :], 1.0).then_inc(s_init, 1)
            pool.wait_ge(s_vec, 16 * 5)
            pool.wait_ge(s_init, 7)
            pool.tensor_tensor(bg[:, 0:2, :], bg_raw[:, 0:2, :], bg_raw[:, 3:5, :], ALU.add).then_inc(s_bg, 1)
            pool.tensor_scalar(bg[:, 2, :], bg_raw[:, 2, :], 1.0, None, ALU.mult).then_inc(s_bg, 1)
            pool.tensor_scalar(bg[:, 3, :], bg_raw[:, 5, :], 1.0, None, ALU.mult).then_inc(s_bg, 1)
            pool.wait_ge(s_bg, 3)
            pool.tensor_scalar(bg[:, 0:2, :], bg[:, 0:2, :], 0.5, None, ALU.mult).then_inc(s_bg, 1)
            pool.wait_ge(s_bg, 4)

            def step(g, i, t, now, ahead, behind, last):
                if now:
                    pool.wait_ge(S["xc_high"], g + 1)
                    pool.tensor_tensor(xcp[1][:], xc[i][:], xcp[0][:].bitcast(F32), ALU.subtract).then_inc(S["xc_low"], 1)
                if behind:
                    pool.wait_ge(S["moments"], GB * g)
                    pool.tensor_tensor(rstd[:, 0, :], moments[:, 0, :, 1], eps[:], ALU.add).then_inc(S["var"], 1)
                    pool.wait_ge(S["var"], g)
                    pool.tensor_tensor(rstd[:, 0, :], rstd[:, 0, :], minus_half[:], ALU.pow).then_inc(S["rstd"], 1)
                if ahead:
                    pool.wait_ge(S["x_high"], g + 2)
                    wait(pool, S["pe_z"], KT * g)
                    pool.tensor_tensor(xp[1 - i][1][:], x[1 - i][:], xp[1 - i][0][:].bitcast(F32), ALU.subtract).then_inc(S["x_low"], 1)
                if last:
                    pool.wait_ge(S["ymoments"], GB * (g - 1))
                    pool.tensor_tensor(rstd[:, 1, :], moments[:, 1, :, 1], eps[:], ALU.add).then_inc(S["yvar"], 1)
                    pool.wait_ge(S["yvar"], g - 1)
                    pool.tensor_tensor(rstd[:, 1, :], rstd[:, 1, :], minus_half[:], ALU.pow).then_inc(S["yrstd"], 1)
                if behind:
                    pool.wait_ge(S["x2"], GB * g)
                    for b in range(GB):
                        pool.tensor_tensor(x2b[1 - i][:, b, :], x2[:, b, :], bl1[:], ALU.add).then_inc(S["x2b"], 1)
                if ahead:
                    pool.wait_ge(S["se"], g + 2)
                    wait(pool, S["pe_dist"], g + 1)
                    pool.tensor_tensor(left[0:SE, :], se[0:SE, :], se[0:SE, :], ALU.add).then_inc(S["left"], 1)
                    pool.tensor_scalar(right[0:SE, :], se[0:SE, :], 1.0, None, ALU.mult).then_inc(S["right"], 1)
                    pool.wait_ge(S["right"], 2 * (g + 1) + 1)
                    pool.tensor_tensor(right[64:64 + SE, :], se[64:64 + SE, :], se[64:64 + SE, :], ALU.mult).then_inc(S["right"], 1)
                    pool.wait_ge(S["right"], 2 * (g + 2))
                if behind:
                    pool.wait_ge(S["adj_high"], g)
                    pool.tensor_tensor(adjp[1][:], adj_o[:], adjp[0][:].bitcast(F32), ALU.subtract).then_inc(S["adj_low"], 1)

            steps(pool, step)

        @block.scalar
        def _(act):
            act.wait_ge(s_vec, 16 * 5)
            act.wait_ge(s_bg, 4)

            def step(g, i, t, now, ahead, behind, last):
                def gate_tanh(k):
                    act.wait_ge(S["pe_r"], KT * g + k + 1)
                    if k == 0:
                        wait(act, S["rn"], KT * g)
                    act.activation(r[:, k, :], gate_banks[k][:], ACT.Tanh, bias=bg[:, 0, k:k + 1], scale=0.5).then_inc(S["r_tanh"], 1)

                def candidate(k):
                    act.wait_ge(S["n_in"], KT * g + k + 1)
                    if k == 0:
                        wait(act, S["nx"], KT * g)
                    act.activation(n[:, k, :], n_in[:, k, :], ACT.Tanh, bias=bg[:, 2, k:k + 1]).then_inc(S["n_done"], 1)

                def z_tanh(k):
                    act.wait_ge(S["pe_z"], KT * g + k + 1)
                    if k == 0:
                        wait(act, S["zdiff"], KT * g)
                    act.activation(z[:, k, :], gate_banks[0 if k == 0 else 2][:], ACT.Tanh, bias=bg[:, 1, k:k + 1], scale=0.5).then_inc(S["z_tanh"], 1)

                if now:
                    act.wait_ge(s_xc[i], 16 * (t + 1))
                    wait(act, S["pe_z"], KT * g)
                    act.activation(xcp[0][:], xc[i][:], ACT.Copy).then_inc(S["xc_high"], 1)
                    gate_tanh(0)
                if ahead:
                    act.wait_ge(s_x[1 - i], 16 * (t + 1 + i))
                    wait(act, S["pe_z"], KT * g)
                    act.activation(xp[1 - i][0][:], x[1 - i][:], ACT.Copy).then_inc(S["x_high"], 1)
                if now:
                    candidate(0)
                    z_tanh(0)
                if behind:
                    for k in range(KT):
                        act.wait_ge(S["pe_x2T"], g)
                        act.activation(x2p[0][:, k, :], work[3 + k][:], ACT.Copy).then_inc(S["x2T_high"], 1)
                if ahead:
                    act.wait_ge(S["pe_se"], g + 2)
                    wait(act, S["left"], 2 * (g + 1))
                    wait(act, S["right"], 2 * (g + 1))
                    act.activation(se[0:SE_ROWS, :], work[2][0:SE_ROWS, :], ACT.Identity, bias=bse[0:SE_ROWS, :]).then_inc(S["se"], 1)
                    for h in range(2):
                        act.wait_ge(S["msg_sum"], KT * (g + 1) + h + 1)
                        act.activation(msgp[0][:, h, :], msg_sum[:, h, :], ACT.Relu).then_inc(S["msg_high"], 1)
                if now:
                    gate_tanh(1)
                if ahead:
                    act.wait_ge(S["pe_dist"], g + 2)
                    act.activation(e[:], work[2][:], ACT.Exp).then_inc(S["e"], 1)
                if behind:
                    act.wait_ge(s_adjo, 16 * g)
                    wait(act, S["pe_out"], g - 1)
                    act.activation(adjp[0][:], adj_o[:], ACT.Copy).then_inc(S["adj_high"], 1)
                    for h in range(2):
                        act.wait_ge(S["pe_sup"], g)
                        act.activation(supp[0][:, 2 * h:2 * h + 2, :].rearrange("p b d -> p (b d)"), work[3 + h][:], ACT.Copy).then_inc(S["sup_high"], 1)
                if now:
                    candidate(1)
                    z_tanh(1)
                if ahead:
                    for k in range(KT):
                        act.wait_ge(S["pe_nmp"], g + 2)
                        act.activation(nmpp[0][:, k, :], work[3 + k][:], ACT.Copy).then_inc(S["nmp_high"], 1)

            steps(act, step)

        @block.vector
        def _(dve):
            dve.wait_ge(s_vec, 16 * 5)
            chain = (s_wd, 0)
            targets = [([p[:] for p in w_msg], D), ([p[:] for p in w_se], SE_ROWS), ([p[:] for p in w_1], D),
                       ([p[:, 0:KT] for p in w_ih], 3 * D), ([p[:, KT:] for p in w_ih], 3 * D), ([p[:] for p in w_hh], 3 * D)]
            for j, (parts, m) in enumerate(targets):
                dve.wait_ge(s_load, 16 * (j + 1))
                chain = rounded_parts(dve, chain, parts[0], parts[1], raw[:, :, 0:m])

            def step(g, i, t, now, ahead, behind, last):
                gate_hn = (1, 2)
                gate_in = (2, 0)

                def reset_and_sum(k):
                    dve.wait_ge(S["r_tanh"], KT * g + k + 1)
                    dve.tensor_scalar(r[:, k, :], r[:, k, :], 0.5, 0.5, ALU.mult, ALU.add).then_inc(S["r_done"], 1)
                    dve.wait_ge(S["r_done"], KT * g + k + 1)
                    dve.wait_ge(S["pe_hn"], KT * g + k + 1)
                    if k == 0:
                        wait(dve, S["n_done"], KT * g)
                    dve.scalar_tensor_tensor(r[:, k, :], gate_banks[gate_hn[k]][:], bg[:, 3, k:k + 1], r[:, k, :], ALU.add, ALU.mult).then_inc(S["rn"], 1)
                    dve.wait_ge(S["rn"], KT * g + k + 1)
                    dve.wait_ge(S["pe_in"], KT * g + k + 1)
                    dve.tensor_tensor(n_in[:, k, :], gate_banks[gate_in[k]][:], r[:, k, :], ALU.add).then_inc(S["n_in"], 1)

                def blend(k, group, i):
                    dve.wait_ge(S["n_done"], KT * group + k + 1)
                    if k == 0:
                        wait(dve, S["pe_uT"], group)
                    dve.tensor_tensor(u[:, k, :], x[i][:, k, :], n[:, k, :], ALU.subtract).then_inc(S["diff"], 1)
                    dve.tensor_tensor(n[:, k, :], x[i][:, k, :], n[:, k, :], ALU.add).then_inc(S["nx"], 1)
                    dve.wait_ge(S["z_tanh"], KT * group + k + 1)
                    dve.tensor_scalar(z[:, k, :], z[:, k, :], 0.5, 0.5, ALU.mult, ALU.add).then_inc(S["z_done"], 1)
                    dve.wait_ge(S["z_done"], KT * group + k + 1)
                    dve.wait_ge(S["diff"], KT * group + k + 1)
                    dve.tensor_tensor(u[:, k, :], z[:, k, :], u[:, k, :], ALU.mult).then_inc(S["zdiff"], 1)
                    dve.wait_ge(S["zdiff"], KT * group + k + 1)
                    dve.wait_ge(S["nx"], KT * group + k + 1)
                    dve.tensor_tensor(u[:, k, :], u[:, k, :], n[:, k, :], ALU.add).then_inc(S["u_done"], 1)

                def norm_stats(which, source, stats_sem, moments_sem, group):
                    for b in range(GB):
                        dve.bn_stats(stats[:, which, b, :], source(b)).then_inc(S[stats_sem], 1)
                    dve.wait_ge(S[stats_sem], GB * (group + 1))
                    dve.memset(carrier[:], 0.0)
                    for b in range(GB):
                        dve.bn_aggr(moments[:, which, b, :], stats[:, which, b, :]).then_inc(S[moments_sem], 1)

                if last:
                    dve.wait_ge(S["pe_out"], g - 1)
                    wait(dve, S["x2b"], GB * (g - 1))
                    wait(dve, S["res"], GB * (g - 2))
                    for h in range(2):
                        dve.tensor_tensor(y[:, 2 * h:2 * h + 2, :].rearrange("p b d -> p (b d)"), work[h][:],
                                          x2b[i][:, 2 * h:2 * h + 2, :].rearrange("p b d -> p (b d)"), ALU.add).then_inc(S["y"], 1)
                    dve.wait_ge(S["y"], 2 * (g - 1))
                    norm_stats(1, lambda b: y[:, b, :], "ystats", "ymoments", g - 2)
                if behind:
                    dve.wait_ge(S["pe_uT"], g)
                    norm_stats(0, lambda b: work[b // 2][:, (b % 2) * D:(b % 2 + 1) * D], "stats", "moments", g - 1)
                if now:
                    reset_and_sum(0)
                if behind:
                    dve.wait_ge(S["rstd"], g)
                    wait(dve, S["pe_x2T"], g - 1)
                    wait(dve, S["x2b"], GB * (g - 1))
                    for b in range(GB):
                        dve.tensor_scalar(x2[:, b, :], work[b // 2][:, (b % 2) * D:(b % 2 + 1) * D],
                                          moments[:, 0, b, 0:1], rstd[:, 0, b:b + 1], ALU.subtract, ALU.mult).then_inc(S["x2"], 1)
                if last:
                    dve.wait_ge(S["yrstd"], g - 1)
                    wait(dve, s_out, 16 * (g - 2))
                    for b in range(GB):
                        dve.tensor_scalar(res[:, b, :], y[:, b, :], moments[:, 1, b, 0:1], rstd[:, 1, b:b + 1],
                                          ALU.subtract, ALU.mult).then_inc(S["res"], 1)
                if now:
                    blend(0, g, i)
                if behind:
                    for k in range(KT):
                        dve.wait_ge(S["x2T_high"], KT * (g - 1) + k + 1)
                        dve.tensor_tensor(x2p[1][:, k, :], work[3 + k][:], x2p[0][:, k, :].bitcast(F32), ALU.subtract).then_inc(S["x2T_low"], 1)
                if ahead:
                    dve.wait_ge(S["pe_msg"], g + 2)
                    wait(dve, S["msg_low"], KT * (g + 1))
                    for h in range(2):
                        dve.tensor_tensor(msg_sum[:, h, :].rearrange("p (b d) -> p b d", b=2),
                                          work[h][:].rearrange("p (b d) -> p b d", b=2),
                                          bmsg_raw[:].unsqueeze(1).to_broadcast([P, 2, D]), ALU.add).then_inc(S["msg_sum"], 1)
                    dve.wait_ge(S["se"], g + 2)
                    wait(dve, S["pe_dist"], g + 1)
                    dve.scalar_tensor_tensor(left[32:32 + SE, :], se[32:32 + SE, :], -1.0, se[32:32 + SE, :], ALU.mult, ALU.mult).then_inc(S["left"], 1)
                    wait(dve, S["pe_nmp"], g + 1)
                    for h in range(2):
                        dve.wait_ge(S["msg_high"], KT * (g + 1) + h + 1)
                        dve.scalar_tensor_tensor(msgp[1][:, h, :], msg_sum[:, h, :], 0.0, msgp[0][:, h, :].bitcast(F32), ALU.max, ALU.subtract).then_inc(S["msg_low"], 1)
                if behind:
                    for h in range(2):
                        dve.wait_ge(S["sup_high"], KT * (g - 1) + h + 1)
                        dve.tensor_tensor(supp[1][:, 2 * h:2 * h + 2, :].rearrange("p b d -> p (b d)"), work[3 + h][:],
                                          supp[0][:, 2 * h:2 * h + 2, :].rearrange("p b d -> p (b d)").bitcast(F32), ALU.subtract).then_inc(S["sup_low"], 1)
                if ahead:
                    dve.wait_ge(S["e"], g + 2)
                    dve.wait_ge(s_adj, 16 * (g + 2))
                    dve.tensor_tensor(a[:], e[:], adj[:], ALU.mult).then_inc(S["a"], 1)
                    dve.wait_ge(S["a"], g + 2)
                    dve.tensor_copy(ap[0][:], a[:]).then_inc(S["a_high"], 1)
                    dve.wait_ge(S["a_high"], g + 2)
                    dve.tensor_tensor(ap[1][:], a[:], ap[0][:].bitcast(F32), ALU.subtract).then_inc(S["a_low"], 1)
                if now:
                    reset_and_sum(1)
                    blend(1, g, i)
                if ahead:
                    for k in range(KT):
                        dve.wait_ge(S["nmp_high"], KT * (g + 1) + k + 1)
                        dve.tensor_tensor(nmpp[1][:, k, :], work[3 + k][:], nmpp[0][:, k, :].bitcast(F32), ALU.subtract).then_inc(S["nmp_low"], 1)

            steps(dve, step)

        @block.tensor
        def _(pe):
            pe.wait_ge(s_wd, 12)
            pe.wait_ge(s_init, 7)
            pe.wait_ge(s_vec, 16 * 5)

            def products(out_, pairs):
                calls = [c for l, r_ in pairs for c in ((l[0], r_[0]), (l[0], r_[1]), (l[1], r_[0]))]
                for j, (l, r_) in enumerate(calls):
                    mm = nc.tensor.matmul(out_, l, r_, start=j == 0, stop=j == len(calls) - 1)
                return mm

            def step(g, i, t, now, ahead, behind, last):
                def weight(w, k, m):
                    return [p[:, k, m * P:(m + 1) * P] for p in w]

                def rows(pair_, k):
                    return [p[:, k, :] for p in pair_]

                def x_terms(m):
                    return [(weight(w_hh, k, m), rows(xp[i], k)) for k in range(KT)]

                def in_terms(m):
                    return ([(weight(w_ih, k, m), rows(xcp, k)) for k in range(KT)]
                            + [(weight(w_ih, KT + k, m), rows(nmpp, k)) for k in range(KT)])

                def gate_r(k):
                    if k == 0:
                        pe.wait_ge(S["xc_low"], g + 1)
                        pe.wait_ge(S["nmp_low"], KT * (g + 1))
                        wait(pe, S["n_in"], KT * g)
                    else:
                        pe.wait_ge(S["rn"], KT * g + 1)
                    products(gate_banks[k][:], x_terms(k) + in_terms(k)).then_inc(S["pe_r"], 1)

                def gate_n(k):
                    if k == 1:
                        pe.wait_ge(S["n_in"], KT * g + 1)
                    else:
                        wait(pe, S["r_tanh"], KT * g)
                    products(gate_banks[1 + k][:], x_terms(2 * KT + k)).then_inc(S["pe_hn"], 1)
                    if k == 1:
                        pe.wait_ge(S["z_tanh"], KT * g + 1)
                    else:
                        wait(pe, S["z_tanh"], KT * g)
                    products(gate_banks[2 * (1 - k)][:], in_terms(2 * KT + k)).then_inc(S["pe_in"], 1)

                def gate_z(k):
                    if k == 0:
                        pe.wait_ge(S["r_tanh"], KT * g + 1)
                    else:
                        pe.wait_ge(S["rn"], KT * g + 2)
                    products(gate_banks[0 if k == 0 else 2][:], x_terms(KT + k) + in_terms(KT + k)).then_inc(S["pe_z"], 1)

                if last:
                    pe.wait_ge(S["sup_low"], KT * (g - 1))
                    pe.wait_ge(S["adj_low"], g - 1)
                    wait(pe, S["msg_sum"], KT * (min(g + 1, GROUPS) if isinstance(g, int) else g + 1))
                    for b in range(GB):
                        cols = slice(b * P, (b + 1) * P)
                        mm = products(work[b // 2][:, (b % 2) * D:(b % 2 + 1) * D],
                                      [([p[:, cols] for p in adjp], [p[:, b, :] for p in supp])])
                    mm.then_inc(S["pe_out"], 1)
                if now:
                    gate_r(0)
                if behind:
                    pe.wait_ge(S["u_done"], KT * g)
                    if last:
                        pe.wait_ge(S["y"], 2 * (g - 1))
                    elif now:
                        pe.wait_ge(S["msg_sum"], KT * (g + 1))
                    for b in range(GB):
                        for k in range(KT):
                            at = (b % 2) * D + k * P
                            mm = nc.tensor.transpose(work[b // 2][:, at:at + P], u[:, k, b * P:(b + 1) * P], ident[:])
                    mm.then_inc(S["pe_uT"], 1)
                if now:
                    gate_n(0)
                    gate_z(0)
                if behind:
                    pe.wait_ge(S["x2"], GB * g)
                    if now:
                        pe.wait_ge(S["nmp_low"], KT * (g + 1))
                    for k in range(KT):
                        for b in range(GB):
                            mm = nc.tensor.transpose(work[3 + k][:, b * P:(b + 1) * P], x2[:, b, k * P:(k + 1) * P], ident[:])
                    mm.then_inc(S["pe_x2T"], 1)
                if ahead:
                    xn = xp[1 - i]
                    pe.wait_ge(S["x_low"], g + 2)
                    wait(pe, S["e"], g + 1)
                    products(work[2][0:SE_ROWS, :], [([p[:, k, :] for p in w_se], rows(xn, k)) for k in range(KT)]).then_inc(S["pe_se"], 1)
                    for b in range(GB):
                        mm = products(work[b // 2][:, (b % 2) * D:(b % 2 + 1) * D],
                                      [([p[:, k, b * P:(b + 1) * P] for p in xn], [p[:, k, :] for p in w_msg]) for k in range(KT)])
                    mm.then_inc(S["pe_msg"], 1)
                if now:
                    gate_r(1)
                if ahead:
                    pe.wait_ge(S["left"], 2 * (g + 2))
                    pe.wait_ge(S["right"], 2 * (g + 2))
                    for b in range(GB):
                        cols = slice(b * P, (b + 1) * P)
                        mm = nc.tensor.matmul(work[2][:, cols], left[0:SE_ROWS, cols], right[0:SE_ROWS, cols], start=True, stop=True)
                    mm.then_inc(S["pe_dist"], 1)
                if behind:
                    pe.wait_ge(S["x2T_low"], KT * g)
                    for b in range(GB):
                        mm = products(work[3 + b // 2][:, (b % 2) * D:(b % 2 + 1) * D],
                                      [([p[:, k, b * P:(b + 1) * P] for p in x2p], [p[:, k, :] for p in w_1]) for k in range(KT)])
                    mm.then_inc(S["pe_sup"], 1)
                if now:
                    gate_n(1)
                    gate_z(1)
                if ahead:
                    pe.wait_ge(S["a_low"], g + 2)
                    pe.wait_ge(S["msg_low"], KT * (g + 2))
                    if behind:
                        pe.wait_ge(S["sup_low"], KT * g)
                    for k in range(KT):
                        for b in range(GB):
                            cols = slice(b * P, (b + 1) * P)
                            d0 = (b % 2) * D + k * P
                            mm = products(work[3 + k][:, cols],
                                          [([p[:, b // 2, d0:d0 + P] for p in msgp], [p[:, cols] for p in ap])])
                    mm.then_inc(S["pe_nmp"], 1)

            steps(pe, step)


def _layouts(inputs):
    import numpy as np

    c = {k: np.asarray(v) for k, v in inputs.items()}
    x, adj = c["x"], c["adj"]
    cols = lambda v: v.reshape(-1, P).T
    norms = [cols(c["L0_gnn_" + name]) for name in ("bn1_g", "bn2_g", "bn1_b", "bn2_b", "bn1_m", "bn2_m", "bn1_v", "bn2_v")]
    gates = [cols(c["L0_gnn_" + name][j * D:(j + 1) * D]) for name in ("b_ih", "b_hh") for j in range(3)]
    gates += [np.zeros_like(gates[0])] * 2
    w_se, b_se = c["L0_gnn_w_se"], c["L0_gnn_b_se"]
    w_seT = np.zeros((D, SE_ROWS), w_se.dtype)
    se_bias = np.zeros((P, 1), b_se.dtype)
    for q in range(3):
        w_seT[:, 32 * q:32 * q + SE] = w_se.T
        se_bias[32 * q:32 * q + SE, 0] = b_se
    return {
        "xT": x.reshape(GROUPS, GB, P, KT, P).transpose(0, 3, 4, 1, 2).reshape(GROUPS, KT, P, COLS),
        "adjT": adj.reshape(GROUPS, GB, P, P).transpose(0, 3, 1, 2).reshape(GROUPS, P, COLS),
        "conv1_wT": c["L0_gnn_conv1_w"][:, :, 0].T.reshape(KT, P, D).transpose(1, 0, 2),
        "conv2_wT": c["L0_gnn_conv2_w"].transpose(1, 2, 0).reshape(KT, P, TAPS * D),
        "bn": np.stack(norms, axis=1),
        "w_seT": w_seT,
        "w_msgT": c["L0_gnn_w_msg"].T,
        "w_ihT": c["L0_gnn_w_ih"].T,
        "w_hhT": c["L0_gnn_w_hh"].T,
        "w_l1": c["L1_gnn_weight"],
        "se_bias": se_bias,
        "msg_bias": np.broadcast_to(c["L0_gnn_b_msg"], (P, D)),
        "gate_bias": np.stack(gates, axis=1),
        "l1_bias": np.broadcast_to(c["L1_gnn_bias"], (P, D)),
        "identity": np.eye(P, dtype=np.float32),
    }


def kernel(**inputs):
    import numpy as np
    import concourse.bacc as bacc
    from concourse.bass_utils import run_bass_kernel_spmd

    nc = bacc.Bacc("TRN2", target_bir_lowering=False, num_devices=1)
    arrays = {name: np.ascontiguousarray(a) for name, a in _layouts(inputs).items()}
    t = {name: nc.dram_tensor(name, a.shape, mybir.dt.from_np(a.dtype), kind="ExternalInput").ap()
         for name, a in arrays.items()}
    out = nc.dram_tensor("out", (GROUPS * GB, P, D), F32, kind="ExternalOutput").ap()
    x_conv = nc.dram_tensor("x_conv", (GROUPS, KT, P, COLS), F32, kind="Internal").ap()
    conv_branch(nc, t["xT"], t["conv1_wT"], t["conv2_wT"], t["bn"], x_conv)
    gated_layer_and_graph_layer(nc, t["xT"], t["adjT"], x_conv, t["w_seT"], t["w_msgT"], t["w_ihT"], t["w_hhT"],
                                t["w_l1"], t["se_bias"], t["msg_bias"], t["gate_bias"], t["l1_bias"],
                                t["identity"], out)
    r = run_bass_kernel_spmd(nc, [arrays], core_ids=[0])
    return r.results[0]["out"]
```

```python
from contextlib import ExitStack

import concourse.bass as bass
from concourse import mybir

F32 = mybir.dt.float32
F32R = mybir.dt.float32r
ALU = mybir.AluOpType
ACT = mybir.ActivationFunctionType

P = 128
KT = 2
D = KT * P
GB = 4
COLS = GB * P
GROUPS = 32
TAPS = 17
PAD = TAPS // 2
EPS = 1e-5
OUTS = 64
WINDOWS = P // OUTS
WINDOW = OUTS + TAPS - 1
FREQS = WINDOW // 2 + 1
ROWS = 2 * FREQS
PAIRS = 2 * GROUPS
STACK = 2 * 32 + TAPS
CHUNK = 4096
CHUNKS = D * D // CHUNK
SE = 3
SE_ROWS = 2 * 32 + SE


def wait(engine, semaphore, count):
    if not isinstance(count, int) or count > 0:
        engine.wait_ge(semaphore, count)


def rounded_parts(engine, chain, high, low, value):
    sem, n = chain
    engine.tensor_copy(high, value).then_inc(sem, 1)
    engine.wait_ge(sem, n + 1)
    engine.tensor_tensor(low, value, high.bitcast(F32), ALU.subtract).then_inc(sem, 1)
    return sem, n + 2


def transform_weights(nc, taps3, tap_dft, weights_f):
    with ExitStack() as ctx:
        def sb(name, shape, dt=F32):
            return ctx.enter_context(nc.sbuf_tensor("tw_" + name, shape, dt))

        def sem(name):
            return ctx.enter_context(nc.semaphore("tw_" + name))

        dft_raw = sb("tap_dft_raw", [STACK, ROWS])
        dft = sb("tap_dft", [STACK, ROWS], F32R)
        raw = [sb(f"taps_raw_{i}", [STACK, CHUNK]) for i in range(2)]
        parts = [sb(f"taps_parts_{i}", [STACK, CHUNK], F32R) for i in range(2)]
        spectrum = [sb(f"spectrum_{i}", [ROWS, CHUNK]) for i in range(2)]
        banks = [ctx.enter_context(nc.psum_tensor(f"tw_wf_{i}", [P, COLS], F32)) for i in range(4)]
        s_dft = sem("dft_loaded")
        s_zero = sem("rows_zeroed")
        s_in = [sem(f"taps_loaded_{i}") for i in range(2)]
        s_round = sem("taps_rounded")
        s_low = sem("taps_low")
        s_dftp = sem("dft_parts")
        s_mm = sem("spectrum_sums")
        s_even = sem("spectrum_even")
        s_odd = sem("spectrum_odd")
        s_st = [sem(f"spectrum_stored_{i}") for i in range(2)]
        block = ctx.enter_context(nc.Block())
        per = CHUNK // COLS

        @block.sync
        def _(sp):
            sp.dma_start(dft_raw[:], tap_dft).then_inc(s_dft, 16)
            sp.wait_ge(s_zero, 2)
            for c in range(CHUNKS):
                i = c % 2
                if c >= 2:
                    sp.wait_ge(s_low, c - 1)
                for q in range(3):
                    sp.dma_start(raw[i][32 * q:32 * q + TAPS, :], taps3[:, c * CHUNK:(c + 1) * CHUNK]).then_inc(s_in[i], 16)

        @block.gpsimd
        def _(pool):
            for i in range(2):
                pool.memset(raw[i][:], 0.0).then_inc(s_zero, 1)
            for c in range(CHUNKS):
                i = c % 2
                pool.wait_ge(s_even, (c + 1) * per // 2)
                pool.wait_ge(s_odd, (c + 1) * per // 2)
                pool.dma_start(weights_f[:, c * CHUNK:(c + 1) * CHUNK], spectrum[i][:]).then_inc(s_st[i], 16)
            for i in range(2):
                pool.wait_ge(s_st[i], 16 * (CHUNKS // 2))

        def copies(engine, half, done):
            def chunk(c, i):
                if c >= 2:
                    engine.wait_ge(s_st[i], 16 * (c // 2))
                for j in range(half, per, 2):
                    engine.wait_ge(s_mm, c * per + j + 1)
                    yield (spectrum[i][:, j * COLS:(j + 1) * COLS], banks[j % 4][0:ROWS, :])
            return chunk

        @block.vector
        def _(dve):
            dve.wait_ge(s_dft, 16)
            dve.tensor_copy(dft[:], dft_raw[:]).then_inc(s_dftp, 1)

            def prepare(c):
                i = c % 2
                dve.wait_ge(s_in[i], 48 * (c // 2 + 1))
                if c >= 2:
                    dve.wait_ge(s_mm, (c - 1) * per)
                dve.tensor_copy(parts[i][:], raw[i][:]).then_inc(s_round, 1)
                dve.wait_ge(s_round, c + 1)
                dve.tensor_tensor(parts[i][64:STACK, :], raw[i][64:STACK, :],
                                  parts[i][64:STACK, :].bitcast(F32), ALU.subtract).then_inc(s_low, 1)

            prepare(0)
            for c in range(CHUNKS):
                if c + 1 < CHUNKS:
                    prepare(c + 1)
                for out_, in_ in copies(dve, 0, s_even)(c, c % 2):
                    dve.tensor_copy(out_, in_).then_inc(s_even, 1)

        @block.scalar
        def _(act):
            for c in range(CHUNKS):
                for out_, in_ in copies(act, 1, s_odd)(c, c % 2):
                    act.activation(out_, in_, ACT.Copy).then_inc(s_odd, 1)

        @block.tensor
        def _(pe):
            pe.wait_ge(s_dftp, 1)
            for c in range(CHUNKS):
                pe.wait_ge(s_low, c + 1)
                for j in range(per):
                    m = c * per + j - 4
                    if m >= 0:
                        pe.wait_ge(s_even if m % 2 == 0 else s_odd, m // 2 + 1)
                    nc.tensor.matmul(banks[j % 4][0:ROWS, :], dft[:], parts[c % 2][:, j * COLS:(j + 1) * COLS],
                                     start=True, stop=True).then_inc(s_mm, 1)


def transform_rows(nc, xT, conv1_wT, bn1_rows, row_dft, spectra):
    with ExitStack() as ctx:
        def sb(name, shape, dt=F32):
            return ctx.enter_context(nc.sbuf_tensor("tr_" + name, shape, dt))

        def sem(name):
            return ctx.enter_context(nc.semaphore("tr_" + name))

        w_raw = sb("conv1_raw", [P, KT, D])
        w = [sb(f"conv1_{part}", [P, KT, D], F32R) for part in ("high", "low")]
        bn = sb("bn1_rows", [P, 4, D])
        half = sb("bn1_half", [P, D])
        bias = sb("bn1_shift", [2 * 32, D], F32R)
        ones_raw = sb("ones_raw", [2 * 32, P])
        ones = sb("ones_rows", [2 * 32, P], F32R)
        dft_raw = sb("row_dft_raw", [P, WINDOWS * ROWS])
        dft = [sb(f"row_dft_{part}", [P, WINDOWS * ROWS], F32R) for part in ("high", "low")]
        x = [sb(f"cx_{i}", [P, KT, COLS]) for i in range(2)]
        xp = [[sb(f"cx_{part}_{i}", [P, KT, 2 * P], F32R) for part in ("high", "low")] for i in range(2)]
        hp = [[sb(f"h_{part}_{i}", [P, 2, D], F32R) for part in ("high", "low")] for i in range(2)]
        c_banks = [ctx.enter_context(nc.psum_tensor(f"tr_c_{i}", [P, 2, D], F32)) for i in range(2)]
        f_banks = [[ctx.enter_context(nc.psum_tensor(f"tr_f_{i}_{k}", [P, COLS], F32)) for k in range(KT)] for i in range(2)]

        s_small = sem("small_loaded")
        s_bn = sem("bn_chain")
        s_w = sem("weights_ready")
        s_ones = sem("ones_ready")
        s_x = [sem(f"cx_loaded_{i}") for i in range(2)]
        s_xh = sem("cx_high")
        s_xl = sem("cx_low")
        s_c = sem("conv1_done")
        s_hh = sem("h_high")
        s_hl = sem("h_low")
        s_f = sem("spectrum_done")
        s_e = sem("spectrum_copied")
        block = ctx.enter_context(nc.Block())

        def pairs(engine, step, first=0, last=PAIRS):
            for q in range(4):
                step(q, q, 0)
            with engine.Fori(1, PAIRS // 4 - 1) as t:
                for j in range(4):
                    step(4 * t + j, j, t)
            for q in range(PAIRS - 4, PAIRS):
                step(q, q % 4, q // 4)

        @block.sync
        def _(sp):
            sp.dma_start(w_raw[:], conv1_wT).then_inc(s_small, 16)
            sp.dma_start(bn[:], bn1_rows).then_inc(s_small, 16)
            sp.dma_start(dft_raw[:], row_dft).then_inc(s_small, 16)

            def load(q, j, t):
                if j % 2 == 0:
                    g, i = (q // 2, j // 2) if isinstance(q, int) else (2 * t + j // 2, j // 2)
                    if not (isinstance(q, int) and q < 4):
                        sp.wait_ge(s_xl, q - 2)
                    sp.dma_start(x[i][:], xT[g].rearrange("k p c -> p k c")).then_inc(s_x[i], 16)

            pairs(sp, load)

        @block.gpsimd
        def _(pool):
            for r in range(2):
                pool.memset(half[:] if r else ones_raw[:], -0.5 if r else 0.0).then_inc(s_ones, 1)
            pool.wait_ge(s_ones, 2)
            for r in range(2):
                pool.memset(ones_raw[32 * r:32 * r + 1, :], 1.0).then_inc(s_ones, 1)
                pool.wait_ge(s_ones, 3 + r)
            pool.wait_ge(s_small, 48)
            chain = [(bn[:, 3, :], bn[:, 3, :], EPS, ALU.add), (bn[:, 3, :], bn[:, 3, :], half[:], ALU.pow),
                     (bn[:, 0, :], bn[:, 0, :], bn[:, 3, :], ALU.mult), (bn[:, 2, :], bn[:, 2, :], bn[:, 0, :], ALU.mult),
                     (bn[:, 1, :], bn[:, 1, :], bn[:, 2, :], ALU.subtract)]
            for n, (out_, a, b, op) in enumerate(chain):
                if n:
                    pool.wait_ge(s_bn, n)
                if n == 0:
                    pool.tensor_scalar(out_, a, b, None, op).then_inc(s_bn, 1)
                else:
                    pool.tensor_tensor(out_, a, b, op).then_inc(s_bn, 1)

            def low_part(q, j, t):
                pool.wait_ge(s_xh, q + 1)
                cols = slice((j % 2) * 2 * P, (j % 2 + 1) * 2 * P)
                pool.tensor_tensor(xp[j % 2][1][:], x[j // 2][:, :, cols], xp[j % 2][0][:].bitcast(F32), ALU.subtract).then_inc(s_xl, 1)

            pairs(pool, low_part)

        @block.scalar
        def _(act):
            def x_high(q, j, t):
                act.wait_ge(s_x[j // 2], 16 * (t + 1))
                if not (isinstance(q, int) and q < 2):
                    act.wait_ge(s_c, q - 1)
                cols = slice((j % 2) * 2 * P, (j % 2 + 1) * 2 * P)
                act.activation(xp[j % 2][0][:], x[j // 2][:, :, cols], ACT.Copy).then_inc(s_xh, 1)

            def h_high(q, j, t):
                act.wait_ge(s_c, q + 1)
                if not (isinstance(q, int) and q < 2):
                    act.wait_ge(s_f, q - 1)
                act.activation(hp[j % 2][0][:], c_banks[j % 2][:], ACT.Relu).then_inc(s_hh, 1)

            x_high(0, 0, 0)
            x_high(1, 1, 0)

            def step(q, j, t):
                if not (isinstance(q, int) and q + 2 >= PAIRS):
                    x_high(q + 2, (j + 2) % 4, t + (j + 2) // 4)
                h_high(q, j, t)

            pairs(act, step)

        @block.vector
        def _(dve):
            dve.wait_ge(s_small, 48)
            dve.wait_ge(s_ones, 4)
            dve.tensor_copy(ones[:], ones_raw[:]).then_inc(s_w, 1)
            chain = rounded_parts(dve, (s_w, 1), dft[0][:], dft[1][:], dft_raw[:])
            dve.wait_ge(s_bn, 5)
            for k in range(KT):
                dve.tensor_tensor(w_raw[:, k], w_raw[:, k], bn[:, 0, :], ALU.mult).then_inc(s_w, 1)
            dve.wait_ge(s_w, 5)
            chain = rounded_parts(dve, (s_w, 5), w[0][:], w[1][:], w_raw[:])
            dve.tensor_copy(bias[:], bn[0:64, 1, :]).then_inc(s_w, 1)
            dve.wait_ge(s_w, 8)
            dve.tensor_tensor(bias[32:64, :], bn[32:64, 1, :], bias[32:64, :].bitcast(F32), ALU.subtract).then_inc(s_w, 1)

            def spectrum(q, j, t):
                if not isinstance(q, int) or q >= 0:
                    i = j % 2
                    dve.wait_ge(s_f, q + 1)
                    for k in range(KT):
                        dve.tensor_scalar(spectra[:, k, :, :, bass.ts(q, 2)].rearrange("p r w b -> p b w r"),
                                          f_banks[i][k][:, 0:2 * WINDOWS * ROWS].rearrange("p (b w r) -> p b w r", b=2, w=WINDOWS),
                                          1.0, None, ALU.mult).then_inc(s_e, 1)

            def step(q, j, t):
                dve.wait_ge(s_hh, q + 1)
                dve.scalar_tensor_tensor(hp[j % 2][1][:].rearrange("p b d -> p (b d)"), c_banks[j % 2][:].rearrange("p b d -> p (b d)"), 0.0,
                                         hp[j % 2][0][:].rearrange("p b d -> p (b d)").bitcast(F32),
                                         ALU.max, ALU.subtract).then_inc(s_hl, 1)
                spectrum(q - 1, (j - 1) % 4, t)

            pairs(dve, step)
            spectrum(PAIRS - 1, 3, 0)

        @block.tensor
        def _(pe):
            def conv1(q, j):
                i = j % 2
                pe.wait_ge(s_xl, q + 1)
                if not (isinstance(q, int) and q < 2):
                    pe.wait_ge(s_hl, q - 1)
                for b in range(2):
                    n = 0
                    for l, r in ((0, 0), (0, 1), (1, 0)):
                        for k in range(KT):
                            nc.tensor.matmul(c_banks[i][:, b, :], xp[i][l][:, k, b * P:(b + 1) * P], w[r][:, k, :],
                                             start=n == 0, stop=False)
                            n += 1
                    mm = nc.tensor.matmul(c_banks[i][:, b, :], ones[:], bias[:], start=False, stop=True)
                mm.then_inc(s_c, 1)

            def dft_of(q, j):
                i = j % 2
                pe.wait_ge(s_hl, q + 1)
                if not (isinstance(q, int) and q < 2):
                    pe.wait_ge(s_e, KT * (q - 1))
                size = WINDOWS * ROWS
                for k in range(KT):
                    for b in range(2):
                        for n, (l, r) in enumerate(((0, 0), (0, 1), (1, 0))):
                            mm = nc.tensor.matmul(f_banks[i][k][:, b * size:(b + 1) * size],
                                                  hp[i][l][:, b, k * P:(k + 1) * P], dft[r][:], start=n == 0, stop=n == 2)
                mm.then_inc(s_f, 1)

            pe.wait_ge(s_w, 9)
            conv1(0, 0)

            def step(q, j, t):
                if not (isinstance(q, int) and q + 1 >= PAIRS):
                    conv1(q + 1, (j + 1) % 4)
                dft_of(q, j)

            pairs(pe, step)


def multiply_spectra(nc, spectra, weights_f, products_f):
    with ExitStack() as ctx:
        def sb(name, shape, dt=F32):
            return ctx.enter_context(nc.sbuf_tensor("ms_" + name, shape, dt))

        def sem(name):
            return ctx.enter_context(nc.semaphore("ms_" + name))

        w_raw = [sb(f"wf_raw_{i}", [P, KT, 2, D]) for i in range(2)]
        w = [[sb(f"wf_{part}_{i}", [P, KT, 2, D], F32R) for part in ("high", "low")] for i in range(2)]
        h = [[sb(f"hf_{part}_{i}", [P, KT, 2, P], F32R) for part in ("high", "low")] for i in range(WINDOWS)]
        b_copy = sb("b_copy", [P, 2, D])
        y = [sb(f"yf_{i}", [P, 2, D]) for i in range(WINDOWS)]
        a_banks = [ctx.enter_context(nc.psum_tensor(f"ms_a_{i}", [P, 2, D], F32)) for i in range(WINDOWS)]
        b_banks = [ctx.enter_context(nc.psum_tensor(f"ms_b_{i}", [P, 2, D], F32)) for i in range(WINDOWS)]

        s_in = [sem(f"wf_loaded_{i}") for i in range(2)]
        s_wh = sem("wf_high")
        s_wl = sem("wf_low")
        s_hh = sem("hf_high")
        s_hl = sem("hf_low")
        s_mm = sem("products_done")
        s_b = sem("b_copied")
        s_y = sem("y_done")
        s_st = [sem(f"y_stored_{i}") for i in range(WINDOWS)]
        block = ctx.enter_context(nc.Block())

        def frequencies(engine, step):
            for f in range(2):
                step(f, f, 0)
            with engine.Fori(1, FREQS // 2 - 1) as t:
                for i in range(2):
                    step(2 * t + i, i, t)
            for f in range(2 * (FREQS // 2 - 1), FREQS):
                step(f, f % 2, f // 2)

        @block.sync
        def _(sp):
            def load(f, i, t):
                if not (isinstance(f, int) and f < 2):
                    sp.wait_ge(s_wl, f - 1)
                for k in range(KT):
                    sp.dma_start(w_raw[i][:, k], weights_f[f, :, k].rearrange("r p o -> p r o")).then_inc(s_in[i], 16)

            load(0, 0, 0)
            load(1, 1, 0)

            def step(f, i, t):
                if not (isinstance(f, int) and f + 2 >= FREQS):
                    load(f + 2, i, t + 1)
                for v in range(WINDOWS):
                    sp.wait_ge(s_y, 2 * (WINDOWS * f + v + 1))
                    sp.dma_start(products_f[:, v, f], y[v][:]).then_inc(s_st[v], 16)

            frequencies(sp, step)
            for v in range(WINDOWS):
                sp.wait_ge(s_st[v], 16 * FREQS)

        @block.gpsimd
        def _(pool):
            def step(f, i, t):
                pool.wait_ge(s_wh, f + 1)
                pool.tensor_tensor(w[i][1][:], w_raw[i][:], w[i][0][:].bitcast(F32), ALU.subtract).then_inc(s_wl, 1)

            frequencies(pool, step)

        @block.scalar
        def _(act):
            def high(f, i, t):
                act.wait_ge(s_in[i], 32 * (t + 1))
                if not (isinstance(f, int) and f < 2):
                    act.wait_ge(s_mm, WINDOWS * (f - 1))
                act.activation(w[i][0][:], w_raw[i][:], ACT.Copy).then_inc(s_wh, 1)

            high(0, 0, 0)

            def step(f, i, t):
                if not (isinstance(f, int) and f + 1 >= FREQS):
                    high(f + 1, 1 - i, t + i)
                for v in range(WINDOWS):
                    act.wait_ge(s_mm, WINDOWS * f + v + 1)
                    wait(act, s_y, 2 * (WINDOWS * f + v))
                    act.activation(b_copy[:], b_banks[v][:], ACT.Copy).then_inc(s_b, 1)

            frequencies(act, step)

        @block.vector
        def _(dve):
            def split(f, v, i):
                n = WINDOWS * f + v
                if not (isinstance(f, int) and f < 1):
                    dve.wait_ge(s_mm, n - WINDOWS + 1)
                source = spectra[:, :, bass.ts(f, 2), v, :]
                dve.tensor_scalar(h[v][0][:], source, 1.0, None, ALU.mult).then_inc(s_hh, 1)
                dve.wait_ge(s_hh, n + 1)
                dve.tensor_tensor(h[v][1][:], source, h[v][0][:].bitcast(F32), ALU.subtract).then_inc(s_hl, 1)

            for v in range(WINDOWS):
                split(0, v, 0)

            def step(f, i, t):
                for v in range(WINDOWS):
                    if not (isinstance(f, int) and f + 1 >= FREQS):
                        split(f + 1, v, 1 - i)
                    n = WINDOWS * f + v
                    dve.wait_ge(s_b, n + 1)
                    if not (isinstance(f, int) and f < 1):
                        dve.wait_ge(s_st[v], 16 * f)
                    dve.tensor_tensor(y[v][:, 0, :], a_banks[v][:, 0, :], b_copy[:, 1, :], ALU.subtract).then_inc(s_y, 1)
                    dve.tensor_tensor(y[v][:, 1, :], a_banks[v][:, 1, :], b_copy[:, 0, :], ALU.add).then_inc(s_y, 1)

            frequencies(dve, step)

        @block.tensor
        def _(pe):
            def step(f, i, t):
                pe.wait_ge(s_wl, f + 1)
                for v in range(WINDOWS):
                    pe.wait_ge(s_hl, WINDOWS * f + v + 1)
                    if not (isinstance(f, int) and f < 1):
                        pe.wait_ge(s_y, 2 * (WINDOWS * (f - 1) + v + 1))
                    for r, bank in ((0, a_banks[v]), (1, b_banks[v])):
                        n = 0
                        for a, b in ((0, 0), (0, 1), (1, 0)):
                            for k in range(KT):
                                mm = nc.tensor.matmul(bank[:], h[v][a][:, k, r, :], w[i][b][:, k], start=n == 0, stop=n == 5)
                                n += 1
                    mm.then_inc(s_mm, 1)

            frequencies(pe, step)


def gated_layer_and_graph_layer(nc, xT, adjT, products_f, inverse_dft, bn2, w_seT, w_msgT, w_ihT, w_hhT, w_l1, se_bias,
                                msg_bias, gate_bias, l1_bias, identity, out):
    with ExitStack() as ctx:
        def sb(name, shape, dt=F32):
            return ctx.enter_context(nc.sbuf_tensor("gl_" + name, shape, dt))

        def sem(name):
            return ctx.enter_context(nc.semaphore("gl_" + name))

        def bank(name):
            return ctx.enter_context(nc.psum_tensor("gl_" + name, [P, COLS], F32))

        def pair(name, shape):
            return [sb(f"{name}_{part}", shape, F32R) for part in ("high", "low")]

        w_se = pair("w_se", [P, KT, SE_ROWS])
        w_msg = pair("w_msg", [P, KT, D])
        w_ih = pair("w_ih", [P, 2 * KT, 3 * D])
        w_hh = pair("w_hh", [P, KT, 3 * D])
        w_1 = pair("w_1", [P, KT, D])
        raw = sb("w_raw", [P, 2 * KT, 2, D])
        ident = sb("ident", [P, P])
        bse = sb("se_bias_rows", [P, 1])
        bmsg_raw = sb("bmsg_raw", [P, D])
        bmsg = sb("bmsg", [2 * 32, D], F32R)
        ones_raw = sb("ones_raw2", [2 * 32, P])
        ones = sb("ones_rows2", [2 * 32, P], F32R)
        inv_raw = sb("inverse_raw", [ROWS, OUTS])
        inv = pair("inverse", [ROWS, OUTS])
        bn_raw = sb("bn2_raw", [P, 4, KT])
        bl1 = sb("bl1", [P, D])
        bg_raw = sb("bg_raw", [P, 8, KT])
        bg = sb("bg", [P, 4, KT])
        minus_half = sb("minus_half2", [P, GB])
        eps = sb("eps", [P, GB])
        carrier = sb("wait_carrier", [P, 1])

        x = [sb(f"x_{i}", [P, KT, COLS]) for i in range(2)]
        xp = [pair(f"x{i}", [P, KT, COLS]) for i in range(2)]
        yf = [raw[0:ROWS, 0:2].rearrange("p b w o -> p (b w) o"),
              raw[0:ROWS, 2:4].rearrange("p b w o -> p (b w) o")]
        yfp = pair("yf", [ROWS, 2 * WINDOWS, D])
        xc = sb("xc", [P, KT, COLS])
        xcp = [pair(f"xc{i}", [P, KT, COLS]) for i in range(2)]
        adj = sb("adj", [P, COLS])
        adj_o = sb("adj_o", [P, COLS])
        adjp = pair("adj", [P, COLS])
        se = sb("se", [P, COLS])
        left = sb("left", [P, COLS])
        right = sb("right", [P, COLS])
        e = sb("e", [P, COLS])
        a = sb("a", [P, COLS])
        ap = pair("a", [P, COLS])
        msgp = pair("msg", [P, KT, COLS])
        nmpp = [pair(f"nmp{i}", [P, KT, COLS]) for i in range(2)]
        r = sb("r", [P, KT, COLS])
        z = sb("zg", [P, KT, COLS])
        n = sb("n", [P, KT, COLS])
        u = sb("u", [P, KT, COLS])
        stats = sb("stats", [P, 2, GB, 6])
        moments = sb("moments", [P, 2, GB, 2])
        rstd = sb("rstd", [P, 2, GB])
        x2 = sb("x2", [P, GB, D])
        x2b = sb("x2b", [P, GB, D])
        x2p = pair("x2", [P, KT, COLS])
        supp = pair("sup", [P, GB, D])
        y = sb("y2", [P, GB, D])
        res = sb("res", [P, GB, D])

        w_stage = raw[:].rearrange("p b w o -> p (b w o)")[:, 0:KT * 3 * D].rearrange("p (k m) -> p k m", k=KT)

        gate_banks = [bank(f"gate_{i}") for i in range(3)]
        work = [bank(f"work_{i}") for i in range(5)]

        s_load = sem("weights_loaded")
        s_vec = sem("vectors_loaded")
        s_wd = sem("weight_parts")
        s_init = sem("constants_ready")
        s_bg = sem("gate_bias_chain")
        s_x = [sem(f"x_loaded_{i}") for i in range(2)]
        s_yf = [sem(f"spectra_loaded_{j}") for j in range(2)]
        s_ones = sem("ones_written")
        s_bn = sem("bn2_chain")
        s_adj = sem("adj_loaded")
        s_adjo = sem("adj_o_loaded")
        names = {}
        for name in ("x_high", "x_low", "yf_high", "yf_low", "xc_sum", "xc", "xc_high", "xc_low", "se", "left", "right", "e", "a", "a_high",
                     "a_low", "adj_high", "adj_low", "msg_high", "msg_low", "nmp_high", "nmp_low",
                     "r_tanh", "r_done", "z_tanh", "z_done", "rn", "n_in", "n_done", "diff", "zdiff", "nx",
                     "u_done", "stats", "moments", "var", "rstd", "x2", "x2b", "x2T_high", "x2T_low",
                     "sup_high", "sup_low", "y", "ystats", "ymoments", "yvar", "yrstd", "res",
                     "pe_se", "pe_msg", "pe_dist", "pe_nmp", "pe_r", "pe_hn", "pe_in", "pe_z",
                     "pe_yf", "pe_uT", "pe_x2T", "pe_sup", "pe_out"):
            names[name] = sem("q_" + name)
        S = names
        s_out = sem("out_stored")
        block = ctx.enter_context(nc.Block())

        def steps(engine, step):
            def at(g, i):
                def has(k):
                    return 0 <= k < GROUPS
                step(g, i, g // 2, has(g), has(g + 1), has(g - 1), has(g - 2))

            for g in (-1, 0, 1):
                at(g, g % 2)
            with engine.Fori(1, GROUPS // 2 - 1) as t:
                for i in range(2):
                    step(2 * t + i, i, t, True, True, True, True)
            for g in range(GROUPS - 2, GROUPS + 2):
                at(g, g % 2)

        @block.sync
        def _(sp):
            weights = [(w_msgT, KT, D), (w_seT, KT, SE_ROWS), (w_l1, KT, D),
                       (w_ihT[0:KT * P], KT, 3 * D), (w_ihT[KT * P:], KT, 3 * D), (w_hhT, KT, 3 * D)]
            for dst, src in ((ident, identity), (bse, se_bias), (bmsg_raw, msg_bias), (bl1, l1_bias),
                             (bg_raw, gate_bias),
                             (inv_raw, inverse_dft), (bn_raw, bn2)):
                sp.dma_start(dst[:], src).then_inc(s_vec, 16)
            for j, (src, k, m) in enumerate(weights):
                if j:
                    sp.wait_ge(s_wd, 2 * j)
                sp.dma_start(w_stage[:, :, 0:m], src.rearrange("(k p) m -> p k m", p=P)).then_inc(s_load, 16)

            def step(g, i, t, now, ahead, behind, last):
                if ahead:
                    for j in range(2):
                        wait(sp, S["yf_low"], 2 * g + j + 1)
                        sp.dma_start(yf[j], products_f[bass.ts(2 * (g + 1) + j, 2)].rearrange("b w f r o -> (f r) (b w) o")).then_inc(s_yf[j], 16)
                    wait(sp, S["u_done"], KT * g)
                    sp.dma_start(x[1 - i][:], xT[g + 1].rearrange("k p c -> p k c")).then_inc(s_x[1 - i], 16)
                    wait(sp, S["a"], g + 1)
                    sp.dma_start(adj[:], adjT[g + 1]).then_inc(s_adj, 16)
                if behind:
                    wait(sp, S["adj_low"], g - 1)
                    sp.dma_start(adj_o[:], adjT[g - 1]).then_inc(s_adjo, 16)
                if last:
                    sp.wait_ge(S["res"], GB * (g - 1))
                    sp.dma_start(out[bass.ts(g - 2, GB)].rearrange("b n d -> n b d"), res[:]).then_inc(s_out, 16)

            sp.wait_ge(s_wd, 12)
            steps(sp, step)
            sp.wait_ge(s_out, 16 * GROUPS)

        @block.gpsimd
        def _(pool):
            pool.memset(ones_raw[:], 0.0).then_inc(s_init, 1)
            pool.memset(left[:], 0.0).then_inc(s_init, 1)
            pool.memset(right[:], 0.0).then_inc(s_init, 1)
            pool.memset(minus_half[:], -0.5).then_inc(s_init, 1)
            pool.memset(eps[:], EPS).then_inc(s_init, 1)
            pool.wait_ge(s_init, 5)
            pool.memset(left[64:64 + SE, :], -1.0).then_inc(s_init, 1)
            pool.wait_ge(s_init, 6)
            pool.memset(right[32:32 + SE, :], 1.0).then_inc(s_init, 1)
            pool.wait_ge(s_vec, 16 * 7)
            pool.wait_ge(s_init, 7)
            for r in range(2):
                pool.memset(ones_raw[32 * r:32 * r + 1, :], 1.0).then_inc(s_ones, 1)
                pool.wait_ge(s_ones, r + 1)
            chain = [(3, 3, eps[:, 0:KT], ALU.add), (3, 3, minus_half[:, 0:KT], ALU.pow), (0, 0, bn_raw[:, 3], ALU.mult),
                     (2, 2, bn_raw[:, 0], ALU.mult), (1, 1, bn_raw[:, 2], ALU.subtract)]
            for n_done, (to, of, other, op) in enumerate(chain):
                pool.tensor_tensor(bn_raw[:, to], bn_raw[:, of], other, op).then_inc(s_bn, 1)
                pool.wait_ge(s_bn, n_done + 1)
            pool.tensor_tensor(bg[:, 0:2, :], bg_raw[:, 0:2, :], bg_raw[:, 3:5, :], ALU.add).then_inc(s_bg, 1)
            pool.tensor_scalar(bg[:, 2, :], bg_raw[:, 2, :], 1.0, None, ALU.mult).then_inc(s_bg, 1)
            pool.tensor_scalar(bg[:, 3, :], bg_raw[:, 5, :], 1.0, None, ALU.mult).then_inc(s_bg, 1)
            pool.wait_ge(s_bg, 3)
            pool.tensor_scalar(bg[:, 0:2, :], bg[:, 0:2, :], 0.5, None, ALU.mult).then_inc(s_bg, 1)
            pool.wait_ge(s_bg, 4)

            def step(g, i, t, now, ahead, behind, last):
                if behind:
                    pool.wait_ge(S["moments"], GB * g)
                    pool.tensor_tensor(rstd[:, 0, :], moments[:, 0, :, 1], eps[:], ALU.add).then_inc(S["var"], 1)
                    pool.wait_ge(S["var"], g)
                    pool.tensor_tensor(rstd[:, 0, :], rstd[:, 0, :], minus_half[:], ALU.pow).then_inc(S["rstd"], 1)
                if ahead:
                    pool.wait_ge(S["x_high"], g + 2)
                    wait(pool, S["pe_z"], KT * g)
                    pool.tensor_tensor(xp[1 - i][1][:], x[1 - i][:], xp[1 - i][0][:].bitcast(F32), ALU.subtract).then_inc(S["x_low"], 1)
                if last:
                    pool.wait_ge(S["ymoments"], GB * (g - 1))
                    pool.tensor_tensor(rstd[:, 1, :], moments[:, 1, :, 1], eps[:], ALU.add).then_inc(S["yvar"], 1)
                    pool.wait_ge(S["yvar"], g - 1)
                    pool.tensor_tensor(rstd[:, 1, :], rstd[:, 1, :], minus_half[:], ALU.pow).then_inc(S["yrstd"], 1)
                if behind:
                    pool.wait_ge(S["x2"], GB * g)
                    wait(pool, S["y"], 2 * (g - 1))
                    for b in range(GB):
                        pool.tensor_tensor(x2b[:, b, :], x2[:, b, :], bl1[:], ALU.add).then_inc(S["x2b"], 1)
                if ahead:
                    pool.wait_ge(S["se"], g + 2)
                    wait(pool, S["pe_dist"], g + 1)
                    pool.tensor_tensor(left[0:SE, :], se[0:SE, :], se[0:SE, :], ALU.add).then_inc(S["left"], 1)
                    pool.tensor_scalar(right[0:SE, :], se[0:SE, :], 1.0, None, ALU.mult).then_inc(S["right"], 1)
                    pool.wait_ge(S["right"], 2 * (g + 1) + 1)
                    pool.tensor_tensor(right[64:64 + SE, :], se[64:64 + SE, :], se[64:64 + SE, :], ALU.mult).then_inc(S["right"], 1)
                    pool.wait_ge(S["right"], 2 * (g + 2))
                if behind:
                    pool.wait_ge(S["adj_high"], g)
                    pool.tensor_tensor(adjp[1][:], adj_o[:], adjp[0][:].bitcast(F32), ALU.subtract).then_inc(S["adj_low"], 1)

                if ahead:
                    pool.wait_ge(S["xc_high"], g + 2)
                    pool.tensor_tensor(xcp[1 - i][1][:], xc[:], xcp[1 - i][0][:].bitcast(F32), ALU.subtract).then_inc(S["xc_low"], 1)

            steps(pool, step)

        @block.scalar
        def _(act):
            act.wait_ge(s_vec, 16 * 7)
            act.wait_ge(s_bg, 4)
            act.wait_ge(s_bn, 5)

            def step(g, i, t, now, ahead, behind, last):
                def gate_tanh(k):
                    act.wait_ge(S["pe_r"], KT * g + k + 1)
                    if k == 0:
                        wait(act, S["n_done"], KT * g)
                    act.activation(r[:, k, :], gate_banks[k][:], ACT.Tanh, bias=bg[:, 0, k:k + 1], scale=0.5).then_inc(S["r_tanh"], 1)

                def spectra_high(j):
                    act.wait_ge(s_yf[j], 16 * (g + 2))
                    wait(act, S["pe_yf"], 2 * (g + 1) + j)
                    act.activation(yfp[0][:], yf[j], ACT.Copy).then_inc(S["yf_high"], 1)

                def candidate(k):
                    act.wait_ge(S["n_in"], KT * g + k + 1)
                    if k == 0:
                        wait(act, S["nx"], KT * g)
                    act.activation(n[:, k, :], r[:, k, :], ACT.Tanh, bias=bg[:, 2, k:k + 1]).then_inc(S["n_done"], 1)

                def z_tanh(k):
                    act.wait_ge(S["pe_z"], KT * g + k + 1)
                    if k == 0:
                        wait(act, S["zdiff"], KT * g)
                    act.activation(z[:, k, :], gate_banks[0 if k == 0 else 2][:], ACT.Tanh, bias=bg[:, 1, k:k + 1], scale=0.5).then_inc(S["z_tanh"], 1)

                if now:
                    gate_tanh(0)
                if ahead:
                    act.wait_ge(s_x[1 - i], 16 * (t + 1 + i))
                    wait(act, S["pe_z"], KT * g)
                    act.activation(xp[1 - i][0][:], x[1 - i][:], ACT.Copy).then_inc(S["x_high"], 1)
                if now:
                    candidate(0)
                    z_tanh(0)
                if ahead:
                    spectra_high(0)
                if behind:
                    for k in range(KT):
                        act.wait_ge(S["pe_x2T"], g)
                        act.activation(x2p[0][:, k, :], work[3 + k][:], ACT.Copy).then_inc(S["x2T_high"], 1)
                if ahead:
                    act.wait_ge(S["pe_se"], g + 2)
                    wait(act, S["left"], 2 * (g + 1))
                    wait(act, S["right"], 2 * (g + 1))
                    act.activation(se[0:SE_ROWS, :], work[2][0:SE_ROWS, :], ACT.Identity, bias=bse[0:SE_ROWS, :]).then_inc(S["se"], 1)
                    for h in range(2):
                        act.wait_ge(S["pe_msg"], g + 2)
                        wait(act, S["pe_nmp"], g + 1)
                        act.activation(msgp[0][:, h, :], work[h][:], ACT.Relu).then_inc(S["msg_high"], 1)
                if now:
                    gate_tanh(1)
                if ahead:
                    act.wait_ge(S["pe_dist"], g + 2)
                    act.activation(e[:], work[2][:], ACT.Exp).then_inc(S["e"], 1)
                if behind:
                    act.wait_ge(s_adjo, 16 * g)
                    wait(act, S["pe_out"], g - 1)
                    act.activation(adjp[0][:], adj_o[:], ACT.Copy).then_inc(S["adj_high"], 1)
                    for h in range(2):
                        act.wait_ge(S["pe_sup"], g)
                        act.activation(supp[0][:, 2 * h:2 * h + 2, :].rearrange("p b d -> p (b d)"), work[3 + h][:], ACT.Copy).then_inc(S["sup_high"], 1)
                if ahead:
                    spectra_high(1)
                if now:
                    candidate(1)
                if ahead:
                    for k in range(KT):
                        act.wait_ge(S["xc_sum"], KT * (g + 1) + k + 1)
                        act.activation(xc[:, k, :], xc[:, k, :], ACT.Relu, bias=bn_raw[:, 1, k:k + 1]).then_inc(S["xc"], 1)
                    act.wait_ge(S["xc"], KT * (g + 2))
                    wait(act, S["pe_z"], KT * g)
                    act.activation(xcp[1 - i][0][:], xc[:], ACT.Copy).then_inc(S["xc_high"], 1)
                    for k in range(KT):
                        act.wait_ge(S["pe_nmp"], g + 2)
                        act.activation(nmpp[1 - i][0][:, k, :], work[3 + k][:], ACT.Copy).then_inc(S["nmp_high"], 1)
                if now:
                    z_tanh(1)

            steps(act, step)

        @block.vector
        def _(dve):
            dve.wait_ge(s_vec, 16 * 7)
            chain = (s_wd, 0)
            targets = [([p[:] for p in w_msg], D), ([p[:] for p in w_se], SE_ROWS), ([p[:] for p in w_1], D),
                       ([p[:, 0:KT] for p in w_ih], 3 * D), ([p[:, KT:] for p in w_ih], 3 * D), ([p[:] for p in w_hh], 3 * D)]
            for j, (parts, m) in enumerate(targets):
                dve.wait_ge(s_load, 16 * (j + 1))
                chain = rounded_parts(dve, chain, parts[0], parts[1], w_stage[:, :, 0:m])
            chain = rounded_parts(dve, chain, inv[0][:], inv[1][:], inv_raw[:])
            dve.wait_ge(s_ones, 2)
            dve.tensor_copy(ones[:], ones_raw[:]).then_inc(s_wd, 1)
            dve.tensor_copy(bmsg[:], bmsg_raw[0:64, :]).then_inc(s_wd, 1)
            dve.wait_ge(s_wd, 16)
            dve.tensor_tensor(bmsg[32:64, :], bmsg_raw[32:64, :], bmsg[32:64, :].bitcast(F32), ALU.subtract).then_inc(s_wd, 1)
            dve.wait_ge(s_bn, 5)

            def step(g, i, t, now, ahead, behind, last):
                gate_hn = (1, 2)
                gate_in = (2, 0)

                def reset_and_sum(k):
                    dve.wait_ge(S["r_tanh"], KT * g + k + 1)
                    dve.tensor_scalar(r[:, k, :], r[:, k, :], 0.5, 0.5, ALU.mult, ALU.add).then_inc(S["r_done"], 1)
                    dve.wait_ge(S["r_done"], KT * g + k + 1)
                    dve.wait_ge(S["pe_hn"], KT * g + k + 1)
                    dve.scalar_tensor_tensor(r[:, k, :], gate_banks[gate_hn[k]][:], bg[:, 3, k:k + 1], r[:, k, :], ALU.add, ALU.mult).then_inc(S["rn"], 1)
                    dve.wait_ge(S["rn"], KT * g + k + 1)
                    dve.wait_ge(S["pe_in"], KT * g + k + 1)
                    dve.tensor_tensor(r[:, k, :], gate_banks[gate_in[k]][:], r[:, k, :], ALU.add).then_inc(S["n_in"], 1)

                def spectra_low(j):
                    dve.wait_ge(S["yf_high"], 2 * (g + 1) + j + 1)
                    dve.tensor_tensor(yfp[1][:], yf[j], yfp[0][:].bitcast(F32), ALU.subtract).then_inc(S["yf_low"], 1)

                def blend(k, group, i):
                    dve.wait_ge(S["n_done"], KT * group + k + 1)
                    if k == 0:
                        wait(dve, S["pe_uT"], group)
                    dve.tensor_tensor(u[:, k, :], x[i][:, k, :], n[:, k, :], ALU.subtract).then_inc(S["diff"], 1)
                    dve.tensor_tensor(n[:, k, :], x[i][:, k, :], n[:, k, :], ALU.add).then_inc(S["nx"], 1)
                    dve.wait_ge(S["z_tanh"], KT * group + k + 1)
                    dve.tensor_scalar(z[:, k, :], z[:, k, :], 0.5, 0.5, ALU.mult, ALU.add).then_inc(S["z_done"], 1)
                    dve.wait_ge(S["z_done"], KT * group + k + 1)
                    dve.wait_ge(S["diff"], KT * group + k + 1)
                    dve.tensor_tensor(u[:, k, :], z[:, k, :], u[:, k, :], ALU.mult).then_inc(S["zdiff"], 1)
                    dve.wait_ge(S["zdiff"], KT * group + k + 1)
                    dve.wait_ge(S["nx"], KT * group + k + 1)
                    dve.tensor_tensor(u[:, k, :], u[:, k, :], n[:, k, :], ALU.add).then_inc(S["u_done"], 1)

                def norm_stats(which, source, stats_sem, moments_sem, group):
                    for b in range(GB):
                        dve.bn_stats(stats[:, which, b, :], source(b)).then_inc(S[stats_sem], 1)
                    dve.wait_ge(S[stats_sem], GB * (group + 1))
                    dve.memset(carrier[:], 0.0)
                    for b in range(GB):
                        dve.bn_aggr(moments[:, which, b, :], stats[:, which, b, :]).then_inc(S[moments_sem], 1)

                if last:
                    dve.wait_ge(S["pe_out"], g - 1)
                    wait(dve, S["x2b"], GB * (g - 1))
                    wait(dve, S["res"], GB * (g - 2))
                    for h in range(2):
                        dve.tensor_tensor(y[:, 2 * h:2 * h + 2, :].rearrange("p b d -> p (b d)"), work[h][:],
                                          x2b[:, 2 * h:2 * h + 2, :].rearrange("p b d -> p (b d)"), ALU.add).then_inc(S["y"], 1)
                    dve.wait_ge(S["y"], 2 * (g - 1))
                    norm_stats(1, lambda b: y[:, b, :], "ystats", "ymoments", g - 2)
                if behind:
                    dve.wait_ge(S["pe_uT"], g)
                    norm_stats(0, lambda b: work[b // 2][:, (b % 2) * D:(b % 2 + 1) * D], "stats", "moments", g - 1)
                if now:
                    reset_and_sum(0)
                if behind:
                    dve.wait_ge(S["rstd"], g)
                    wait(dve, S["pe_x2T"], g - 1)
                    wait(dve, S["x2b"], GB * (g - 1))
                    for b in range(GB):
                        dve.tensor_scalar(x2[:, b, :], work[b // 2][:, (b % 2) * D:(b % 2 + 1) * D],
                                          moments[:, 0, b, 0:1], rstd[:, 0, b:b + 1], ALU.subtract, ALU.mult).then_inc(S["x2"], 1)
                if last:
                    dve.wait_ge(S["yrstd"], g - 1)
                    wait(dve, s_out, 16 * (g - 2))
                    for b in range(GB):
                        dve.tensor_scalar(res[:, b, :], y[:, b, :], moments[:, 1, b, 0:1], rstd[:, 1, b:b + 1],
                                          ALU.subtract, ALU.mult).then_inc(S["res"], 1)
                if now:
                    blend(0, g, i)
                if behind:
                    for k in range(KT):
                        dve.wait_ge(S["x2T_high"], KT * (g - 1) + k + 1)
                        dve.tensor_tensor(x2p[1][:, k, :], work[3 + k][:], x2p[0][:, k, :].bitcast(F32), ALU.subtract).then_inc(S["x2T_low"], 1)
                if ahead:
                    spectra_low(0)
                    dve.wait_ge(S["se"], g + 2)
                    wait(dve, S["pe_dist"], g + 1)
                    dve.scalar_tensor_tensor(left[32:32 + SE, :], se[32:32 + SE, :], -1.0, se[32:32 + SE, :], ALU.mult, ALU.mult).then_inc(S["left"], 1)
                    for h in range(2):
                        dve.wait_ge(S["msg_high"], KT * (g + 1) + h + 1)
                        dve.scalar_tensor_tensor(msgp[1][:, h, :], work[h][:], 0.0, msgp[0][:, h, :].bitcast(F32), ALU.max, ALU.subtract).then_inc(S["msg_low"], 1)
                if behind:
                    for h in range(2):
                        dve.wait_ge(S["sup_high"], KT * (g - 1) + h + 1)
                        dve.tensor_tensor(supp[1][:, 2 * h:2 * h + 2, :].rearrange("p b d -> p (b d)"), work[3 + h][:],
                                          supp[0][:, 2 * h:2 * h + 2, :].rearrange("p b d -> p (b d)").bitcast(F32), ALU.subtract).then_inc(S["sup_low"], 1)
                if ahead:
                    dve.wait_ge(S["e"], g + 2)
                    dve.wait_ge(s_adj, 16 * (g + 2))
                    dve.tensor_tensor(a[:], e[:], adj[:], ALU.mult).then_inc(S["a"], 1)
                    dve.wait_ge(S["a"], g + 2)
                    dve.tensor_copy(ap[0][:], a[:]).then_inc(S["a_high"], 1)
                    dve.wait_ge(S["a_high"], g + 2)
                    dve.tensor_tensor(ap[1][:], a[:], ap[0][:].bitcast(F32), ALU.subtract).then_inc(S["a_low"], 1)
                if ahead:
                    spectra_low(1)
                if now:
                    reset_and_sum(1)
                if ahead:
                    dve.wait_ge(S["pe_yf"], 2 * (g + 2))
                    wait(dve, S["xc_low"], g + 1)
                    dve.wait_ge(S["x_high"], g + 2)
                    for k in range(KT):
                        dve.scalar_tensor_tensor(xc[:, k, :], work[k][:], bn_raw[:, 0, k:k + 1], x[1 - i][:, k, :], ALU.mult, ALU.add).then_inc(S["xc_sum"], 1)
                    for k in range(KT):
                        dve.wait_ge(S["nmp_high"], KT * (g + 1) + k + 1)
                        dve.tensor_tensor(nmpp[1 - i][1][:, k, :], work[3 + k][:], nmpp[1 - i][0][:, k, :].bitcast(F32), ALU.subtract).then_inc(S["nmp_low"], 1)
                if now:
                    blend(1, g, i)

            steps(dve, step)

        @block.tensor
        def _(pe):
            pe.wait_ge(s_wd, 17)
            pe.wait_ge(s_init, 7)
            pe.wait_ge(s_vec, 16 * 7)

            def products(out_, pairs, more=False):
                calls = [c for l, r_ in pairs for c in ((l[0], r_[0]), (l[0], r_[1]), (l[1], r_[0]))]
                for j, (l, r_) in enumerate(calls):
                    mm = nc.tensor.matmul(out_, l, r_, start=j == 0, stop=j == len(calls) - 1 and not more)
                return mm

            def step(g, i, t, now, ahead, behind, last):
                def weight(w, k, m):
                    return [p[:, k, m * P:(m + 1) * P] for p in w]

                def rows(pair_, k):
                    return [p[:, k, :] for p in pair_]

                def x_terms(m):
                    return [(weight(w_hh, k, m), rows(xp[i], k)) for k in range(KT)]

                def in_terms(m):
                    return ([(weight(w_ih, k, m), rows(xcp[i], k)) for k in range(KT)]
                            + [(weight(w_ih, KT + k, m), rows(nmpp[i], k)) for k in range(KT)])

                def gate_r(k):
                    if k == 0:
                        pe.wait_ge(S["xc_low"], g + 1)
                        pe.wait_ge(S["nmp_low"], KT * (g + 1))
                        wait(pe, S["n_in"], KT * g)
                    else:
                        pe.wait_ge(S["rn"], KT * g + 1)
                    products(gate_banks[k][:], x_terms(k) + in_terms(k)).then_inc(S["pe_r"], 1)

                def gate_n(k):
                    if k == 1:
                        pe.wait_ge(S["n_in"], KT * g + 1)
                    else:
                        wait(pe, S["r_tanh"], KT * g)
                    products(gate_banks[1 + k][:], x_terms(2 * KT + k)).then_inc(S["pe_hn"], 1)
                    if k == 1:
                        pe.wait_ge(S["z_tanh"], KT * g + 1)
                    else:
                        wait(pe, S["z_tanh"], KT * g)
                    products(gate_banks[2 * (1 - k)][:], in_terms(2 * KT + k)).then_inc(S["pe_in"], 1)

                def gate_z(k):
                    if k == 0:
                        pe.wait_ge(S["r_tanh"], KT * g + 1)
                    else:
                        pe.wait_ge(S["rn"], KT * g + 2)
                    products(gate_banks[0 if k == 0 else 2][:], x_terms(KT + k) + in_terms(KT + k)).then_inc(S["pe_z"], 1)

                def transform_back(j):
                    if j == 0:
                        pe.wait_ge(S["msg_low"], KT * (g + 2))
                    pe.wait_ge(S["yf_low"], 2 * (g + 1) + j + 1)
                    for k in range(KT):
                        for b in range(2):
                            for v in range(WINDOWS):
                                at = (2 * j + b) * P + v * OUTS
                                mm = products(work[k][:, at:at + OUTS],
                                              [([p[:, WINDOWS * b + v, k * P:(k + 1) * P] for p in yfp], [p[:] for p in inv])])
                    mm.then_inc(S["pe_yf"], 1)

                if last:
                    pe.wait_ge(S["sup_low"], KT * (g - 1))
                    pe.wait_ge(S["adj_low"], g - 1)
                    wait(pe, S["xc_sum"], KT * (min(g + 1, GROUPS) if isinstance(g, int) else g + 1))
                    for b in range(GB):
                        cols = slice(b * P, (b + 1) * P)
                        mm = products(work[b // 2][:, (b % 2) * D:(b % 2 + 1) * D],
                                      [([p[:, cols] for p in adjp], [p[:, b, :] for p in supp])])
                    mm.then_inc(S["pe_out"], 1)
                if now:
                    gate_r(0)
                if behind:
                    pe.wait_ge(S["u_done"], KT * g)
                    if last:
                        pe.wait_ge(S["y"], 2 * (g - 1))
                    elif now:
                        pe.wait_ge(S["xc_sum"], KT * (g + 1))
                    for b in range(GB):
                        for k in range(KT):
                            at = (b % 2) * D + k * P
                            mm = nc.tensor.transpose(work[b // 2][:, at:at + P], u[:, k, b * P:(b + 1) * P], ident[:])
                    mm.then_inc(S["pe_uT"], 1)
                if now:
                    gate_n(0)
                    gate_z(0)
                if behind:
                    pe.wait_ge(S["x2"], GB * g)
                    if now:
                        pe.wait_ge(S["nmp_low"], KT * (g + 1))
                    for k in range(KT):
                        for b in range(GB):
                            mm = nc.tensor.transpose(work[3 + k][:, b * P:(b + 1) * P], x2[:, b, k * P:(k + 1) * P], ident[:])
                    mm.then_inc(S["pe_x2T"], 1)
                if ahead:
                    xn = xp[1 - i]
                    pe.wait_ge(S["x_low"], g + 2)
                    wait(pe, S["e"], g + 1)
                    products(work[2][0:SE_ROWS, :], [([p[:, k, :] for p in w_se], rows(xn, k)) for k in range(KT)]).then_inc(S["pe_se"], 1)
                    if not behind:
                        wait(pe, S["xc_sum"], KT * (g + 1))
                    for b in range(GB):
                        to = work[b // 2][:, (b % 2) * D:(b % 2 + 1) * D]
                        products(to, [([p[:, k, b * P:(b + 1) * P] for p in xn], [p[:, k, :] for p in w_msg]) for k in range(KT)], more=True)
                        mm = nc.tensor.matmul(to, ones[:], bmsg[:], start=False, stop=True)
                    mm.then_inc(S["pe_msg"], 1)
                if now:
                    gate_r(1)
                if ahead:
                    pe.wait_ge(S["left"], 2 * (g + 2))
                    pe.wait_ge(S["right"], 2 * (g + 2))
                    for b in range(GB):
                        cols = slice(b * P, (b + 1) * P)
                        mm = nc.tensor.matmul(work[2][:, cols], left[0:SE_ROWS, cols], right[0:SE_ROWS, cols], start=True, stop=True)
                    mm.then_inc(S["pe_dist"], 1)
                if behind:
                    pe.wait_ge(S["x2T_low"], KT * g)
                    for b in range(GB):
                        mm = products(work[3 + b // 2][:, (b % 2) * D:(b % 2 + 1) * D],
                                      [([p[:, k, b * P:(b + 1) * P] for p in x2p], [p[:, k, :] for p in w_1]) for k in range(KT)])
                    mm.then_inc(S["pe_sup"], 1)
                if ahead:
                    transform_back(0)
                if now:
                    gate_n(1)
                if ahead:
                    transform_back(1)
                    pe.wait_ge(S["a_low"], g + 2)
                    pe.wait_ge(S["msg_low"], KT * (g + 2))
                    if behind:
                        pe.wait_ge(S["sup_low"], KT * g)
                    for k in range(KT):
                        for b in range(GB):
                            cols = slice(b * P, (b + 1) * P)
                            d0 = (b % 2) * D + k * P
                            mm = products(work[3 + k][:, cols],
                                          [([p[:, b // 2, d0:d0 + P] for p in msgp], [p[:, cols] for p in ap])])
                    mm.then_inc(S["pe_nmp"], 1)
                if now:
                    gate_z(1)

            steps(pe, step)


def _fourier_constants():
    import numpy as np

    f = np.arange(FREQS)

    def waves(at, sign):
        angle = 2 * np.pi * ((at[:, None] * f) % WINDOW) / WINDOW
        return np.stack([np.cos(angle), sign * np.sin(angle)], axis=2).reshape(len(at), ROWS)

    taps = waves(np.arange(TAPS), 1)
    bits = taps.astype(np.float32).view(np.uint32) & np.uint32(0xFFFFF000)
    high = bits.view(np.float32)
    tap_dft = np.zeros((STACK, ROWS), np.float32)
    tap_dft[0:TAPS] = tap_dft[64:64 + TAPS] = high
    tap_dft[32:32 + TAPS] = taps - high
    row_dft = np.zeros((P, WINDOWS, ROWS))
    for w in range(WINDOWS):
        at = np.arange(P) - (w * OUTS - PAD)
        inside = (at >= 0) & (at < WINDOW)
        row_dft[inside, w] = waves(at[inside], -1)
    weight = np.full(FREQS, 2.0)
    weight[[0, -1]] = 1.0
    inverse = waves(np.arange(OUTS), -1).T * np.repeat(weight, 2)[:, None] / WINDOW
    return {"tap_dft": tap_dft, "row_dft": row_dft.reshape(P, -1).astype(np.float32),
            "inverse_dft": inverse.astype(np.float32)}


def _layouts(inputs):
    import numpy as np

    c = {k: np.asarray(v) for k, v in inputs.items()}
    x, adj = c["x"], c["adj"]
    cols = lambda v: v.reshape(-1, P).T
    bn1 = [np.broadcast_to(c["L0_gnn_bn1_" + name], (P, D)) for name in "gbmv"]
    bn2 = [cols(c["L0_gnn_bn2_" + name]) for name in "gbmv"]
    gates = [cols(c["L0_gnn_" + name][j * D:(j + 1) * D]) for name in ("b_ih", "b_hh") for j in range(3)]
    gates += [np.zeros_like(gates[0])] * 2
    w_se, b_se = c["L0_gnn_w_se"], c["L0_gnn_b_se"]
    w_seT = np.zeros((D, SE_ROWS), w_se.dtype)
    se_bias = np.zeros((P, 1), b_se.dtype)
    for q in range(3):
        w_seT[:, 32 * q:32 * q + SE] = w_se.T
        se_bias[32 * q:32 * q + SE, 0] = b_se
    return {
        "xT": x.reshape(GROUPS, GB, P, KT, P).transpose(0, 3, 4, 1, 2).reshape(GROUPS, KT, P, COLS),
        "adjT": adj.reshape(GROUPS, GB, P, P).transpose(0, 3, 1, 2).reshape(GROUPS, P, COLS),
        "conv1_wT": c["L0_gnn_conv1_w"][:, :, 0].T.reshape(KT, P, D).transpose(1, 0, 2),
        "taps": c["L0_gnn_conv2_w"].transpose(2, 1, 0).reshape(TAPS, D * D),
        "bn1_rows": np.stack(bn1, axis=1),
        "bn2": np.stack(bn2, axis=1),
        "w_seT": w_seT,
        "w_msgT": c["L0_gnn_w_msg"].T,
        "w_ihT": c["L0_gnn_w_ih"].T,
        "w_hhT": c["L0_gnn_w_hh"].T,
        "w_l1": c["L1_gnn_weight"],
        "se_bias": se_bias,
        "msg_bias": np.broadcast_to(c["L0_gnn_b_msg"], (P, D)),
        "gate_bias": np.stack(gates, axis=1),
        "l1_bias": np.broadcast_to(c["L1_gnn_bias"], (P, D)),
        "identity": np.eye(P, dtype=np.float32),
        **_fourier_constants(),
    }


def kernel(**inputs):
    import numpy as np
    import concourse.bacc as bacc
    from concourse.bass_utils import run_bass_kernel_spmd

    nc = bacc.Bacc("TRN2", target_bir_lowering=False, num_devices=1)
    arrays = {name: np.ascontiguousarray(a) for name, a in _layouts(inputs).items()}
    t = {name: nc.dram_tensor(name, a.shape, mybir.dt.from_np(a.dtype), kind="ExternalInput").ap()
         for name, a in arrays.items()}
    out = nc.dram_tensor("out", (GROUPS * GB, P, D), F32, kind="ExternalOutput").ap()
    weights_f = nc.dram_tensor("weights_f", (ROWS, D * D), F32, kind="Internal").ap()
    products_f = nc.dram_tensor("products_f", (GROUPS * GB, WINDOWS, FREQS, 2, D), F32, kind="Internal").ap()
    transform_weights(nc, t["taps"], t["tap_dft"], weights_f)
    with nc.sbuf_tensor("spectra", [P, KT, ROWS, WINDOWS, P], F32) as spectra:
        transform_rows(nc, t["xT"], t["conv1_wT"], t["bn1_rows"], t["row_dft"], spectra)
        multiply_spectra(nc, spectra, weights_f.rearrange("(f r) (k p o) -> f r k p o", r=2, k=KT, p=P), products_f)
    gated_layer_and_graph_layer(nc, t["xT"], t["adjT"], products_f, t["inverse_dft"], t["bn2"], t["w_seT"],
                                t["w_msgT"], t["w_ihT"], t["w_hhT"], t["w_l1"], t["se_bias"], t["msg_bias"],
                                t["gate_bias"], t["l1_bias"], t["identity"], out)
    r = run_bass_kernel_spmd(nc, [arrays], core_ids=[0])
    return r.results[0]["out"]
```

```python
from contextlib import ExitStack

import concourse.bass as bass
from concourse import mybir

F32 = mybir.dt.float32
F32R = mybir.dt.float32r
ALU = mybir.AluOpType
ACT = mybir.ActivationFunctionType

P = 128
KT = 2
D = KT * P
GB = 4
COLS = GB * P
GROUPS = 32
TAPS = 17
PAD = TAPS // 2
EPS = 1e-5
OUTS = 64
WINDOWS = P // OUTS
WINDOW = OUTS + TAPS - 1
FREQS = WINDOW // 2
ROWS = 2 * FREQS
PAIRS = 2 * GROUPS
TAP_ROWS = TAPS + 1
STACK = 2 * 32 + TAP_ROWS
UNIT = D * D // PAIRS
SETUP = 12
SE = 3
SE_ROWS = 2 * 32 + SE


def wait(engine, semaphore, count):
    if not isinstance(count, int) or count > 0:
        engine.wait_ge(semaphore, count)


def rounded_parts(engine, chain, high, low, value):
    sem, n = chain
    engine.tensor_copy(high, value).then_inc(sem, 1)
    engine.wait_ge(sem, n + 1)
    engine.tensor_tensor(low, value, high.bitcast(F32), ALU.subtract).then_inc(sem, 1)
    return sem, n + 2


def transform_weights_and_rows(nc, taps, tap_dft, xT, conv1_wT, bn1, identity, row_dft, weights_f, spectra):
    with ExitStack() as ctx:
        def sb(name, shape, dt=F32):
            return ctx.enter_context(nc.sbuf_tensor("tr_" + name, shape, dt))

        def sem(name):
            return ctx.enter_context(nc.semaphore("tr_" + name))

        def bank(name):
            return ctx.enter_context(nc.psum_tensor("tr_" + name, [P, COLS], F32))

        w = [sb(f"conv1_{part}", [P, KT, D], F32R) for part in ("high", "low")]
        bn = sb("bn1", [P, 6, KT])
        bias = sb("bn1_shift", [2 * 32, D], F32R)
        ones = sb("ones_rows", [2 * 32, P], F32R)
        dft = [sb(f"row_dft_{part}", [P, WINDOWS * ROWS], F32R) for part in ("high", "low")]
        tdft = sb("tap_dft", [STACK, ROWS], F32R)
        x = [sb(f"x_{i}", [P, KT, 2 * P]) for i in range(2)]
        xp = [[sb(f"x_{part}_{i}", [P, KT, 2 * P], F32R) for part in ("high", "low")] for i in range(2)]
        hp = [[sb(f"h_{part}_{i}", [P, 2, D], F32R) for part in ("high", "low")] for i in range(2)]
        shared = sb("shared", [P, 2 * UNIT])
        raw = [shared[0:STACK, i * UNIT:(i + 1) * UNIT] for i in range(2)]
        tp = [sb(f"taps_parts_{i}", [STACK, COLS], F32R) for i in range(2)]
        spectrum = [sb(f"taps_spectrum_{i}", [ROWS, UNIT]) for i in range(2)]
        c_banks = [bank(f"conv1_{i}") for i in range(2)]
        f_banks = [bank(f"rows_{k}") for k in range(KT)]
        t_banks = [bank(f"taps_{i}") for i in range(2)]
        b_bank = bank("broadcast")

        at = 0
        views = []
        for size in (KT * D, WINDOWS * ROWS, P, P, 2 * D, ROWS):
            views.append(shared[:, at:at + size])
            at += size
        w_raw, dft_raw, ident, all_ones, diag, tdft_raw = views
        w_raw = w_raw.rearrange("p (k d) -> p k d", k=KT)

        s_small = sem("small_loaded")
        s_pool = sem("pool_setup")
        s_bn = sem("bn_chain")
        s_diag = sem("diagonals_ready")
        s_bc = sem("rows_broadcast")
        s_w = sem("weights_ready")
        s_zero = sem("raw_zeroed")
        s_x = [sem(f"x_loaded_{i}") for i in range(2)]
        s_t = [sem(f"taps_loaded_{i}") for i in range(2)]
        s_xh = sem("x_high")
        s_xl = sem("x_low")
        s_th = sem("taps_high")
        s_tl = sem("taps_low")
        s_tm = sem("taps_transformed")
        s_te = sem("taps_spectrum_copied")
        s_ts = [sem(f"taps_spectrum_stored_{i}") for i in range(2)]
        s_c = sem("conv1_done")
        s_hh = sem("h_high")
        s_hl = sem("h_low")
        s_f = sem("spectrum_done")
        s_e = sem("spectrum_copied")
        block = ctx.enter_context(nc.Block())

        def pairs(engine, step):
            for q in range(4):
                step(q, q, 0)
            with engine.Fori(1, PAIRS // 4 - 1) as t:
                for j in range(4):
                    step(4 * t + j, j, t)
            for q in range(PAIRS - 4, PAIRS):
                step(q, q % 4, q // 4)

        def later(q, n):
            return not isinstance(q, int) or q >= n

        @block.sync
        def _(sp):
            for dst, src in ((w_raw, conv1_wT), (bn[:, 0:4], bn1), (dft_raw, row_dft), (ident, identity),
                             (tdft_raw[0:STACK], tap_dft)):
                sp.dma_start(dst, src).then_inc(s_small, 16)

            def load_x(q, j, t):
                if later(q, 2):
                    sp.wait_ge(s_xl, q - 1)
                cols = slice((j % 2) * 2 * P, (j % 2 + 1) * 2 * P)
                sp.dma_start(x[j % 2][:], xT[2 * t + j // 2][:, :, cols].rearrange("k p c -> p k c")).then_inc(s_x[j % 2], 16)

            def load_taps(q, j, t):
                if later(q, 2):
                    sp.wait_ge(s_tl, 2 * (q - 1))
                for copy in range(3):
                    sp.dma_start(raw[j % 2][32 * copy:32 * copy + TAP_ROWS, :], taps[:, bass.ts(q, UNIT)]).then_inc(s_t[j % 2], 16)

            for q in range(2):
                load_x(q, q, 0)
            for q in range(2, 4):
                load_x(q, q, 0)
            sp.wait_ge(s_zero, 1)
            load_taps(0, 0, 0)
            load_taps(1, 1, 0)

            def step(q, j, t):
                if not isinstance(q, int) or q + 2 < PAIRS:
                    load_taps(q + 2, (j + 2) % 4, t + (j + 2) // 4)
                if not isinstance(q, int) or q + 4 < PAIRS:
                    load_x(q + 4, j, t + 1)
                sp.wait_ge(s_te, 2 * (q + 1))
                sp.dma_start(weights_f[:, bass.ts(q, UNIT)], spectrum[j % 2][:]).then_inc(s_ts[j % 2], 16)

            pairs(sp, step)
            for i in range(2):
                sp.wait_ge(s_ts[i], 16 * (PAIRS // 2))

        @block.gpsimd
        def _(pool):
            pool.memset(all_ones, 1.0).then_inc(s_pool, 1)
            pool.memset(bn[:, 4, :], EPS).then_inc(s_pool, 1)
            pool.memset(bn[:, 5, :], -0.5).then_inc(s_pool, 1)
            pool.wait_ge(s_pool, 3)
            pool.wait_ge(s_small, 16 * 5)
            for n, (to, of, other, op) in enumerate(((3, 3, 4, ALU.add), (3, 3, 5, ALU.pow), (0, 0, 3, ALU.mult),
                                                     (2, 2, 0, ALU.mult), (1, 1, 2, ALU.subtract))):
                pool.tensor_tensor(bn[:, to], bn[:, of], bn[:, other], op).then_inc(s_bn, 1)
                pool.wait_ge(s_bn, n + 1)

            def x_low(q, j):
                pool.wait_ge(s_xh, q + 1)
                pool.tensor_tensor(xp[j % 2][1][:], x[j % 2][:], xp[j % 2][0][:].bitcast(F32), ALU.subtract).then_inc(s_xl, 1)

            x_low(0, 0)
            x_low(1, 1)
            pool.wait_ge(s_w, SETUP)
            pool.memset(shared[:], 0.0).then_inc(s_zero, 1)
            pool.wait_ge(s_zero, 1)

            def step(q, j, t):
                if not isinstance(q, int) or q + 2 < PAIRS:
                    x_low(q + 2, (j + 2) % 4)

            pairs(pool, step)

        @block.scalar
        def _(act):
            def x_high(q, j, t):
                act.wait_ge(s_x[j % 2], 16 * (2 * t + j // 2 + 1))
                if later(q, 2):
                    act.wait_ge(s_c, q - 1)
                act.activation(xp[j % 2][0][:], x[j % 2][:], ACT.Copy).then_inc(s_xh, 1)

            def taps_high(q, j, t):
                act.wait_ge(s_t[j % 2], 48 * (2 * t + j // 2 + 1))
                for half in range(2):
                    if later(q, 1):
                        act.wait_ge(s_tm, 2 * (q - 1) + half + 1)
                    act.activation(tp[half][:], raw[j % 2][:, half * COLS:(half + 1) * COLS], ACT.Copy).then_inc(s_th, 1)

            x_high(0, 0, 0)
            x_high(1, 1, 0)

            def step(q, j, t):
                act.wait_ge(s_c, q + 1)
                if later(q, 2):
                    act.wait_ge(s_f, KT * (q - 1))
                act.activation(hp[j % 2][0][:].rearrange("p b d -> p (b d)"), c_banks[j % 2][:], ACT.Relu).then_inc(s_hh, 1)
                if not isinstance(q, int) or q + 2 < PAIRS:
                    x_high(q + 2, (j + 2) % 4, t + (j + 2) // 4)
                if not later(q, 1):
                    taps_high(q, j, t)
                if later(q, 2):
                    act.wait_ge(s_ts[j % 2], 16 * (2 * t + j // 2))
                for half in range(2):
                    act.wait_ge(s_tm, 2 * q + half + 1)
                    act.activation(spectrum[j % 2][:, half * COLS:(half + 1) * COLS], t_banks[half][0:ROWS, :], ACT.Copy).then_inc(s_te, 1)
                if not isinstance(q, int) or q + 1 < PAIRS:
                    taps_high(q + 1, (j + 1) % 4, t + (j + 1) // 4)

            pairs(act, step)

        @block.vector
        def _(dve):
            dve.wait_ge(s_pool, 3)
            dve.wait_ge(s_bn, 5)
            for n in range(2):
                for k in range(KT):
                    at_ = n * D + k * P
                    dve.tensor_scalar(diag[:, at_:at_ + P], ident, bn[:, n, k:k + 1], None, ALU.mult).then_inc(s_diag, 1)
            chain = rounded_parts(dve, (s_w, 0), dft[0][:], dft[1][:], dft_raw)
            dve.tensor_copy(tdft[:], tdft_raw[0:STACK]).then_inc(s_w, 1)
            dve.memset(ones[:].bitcast(F32), 0.0).then_inc(s_w, 1)
            dve.wait_ge(s_w, 4)
            for row in (0, 32):
                dve.tensor_copy(ones[row:row + 1, :], all_ones[row:row + 1, :]).then_inc(s_w, 1)
            dve.wait_ge(s_bc, 1)
            for k in range(KT):
                dve.tensor_tensor(w_raw[:, k], w_raw[:, k], b_bank[:, 0:D], ALU.mult).then_inc(s_w, 1)
            dve.tensor_copy(bias[:], b_bank[0:64, D:2 * D]).then_inc(s_w, 1)
            dve.wait_ge(s_w, 9)
            dve.tensor_tensor(bias[32:64, :], b_bank[32:64, D:2 * D], bias[32:64, :].bitcast(F32), ALU.subtract).then_inc(s_w, 1)
            chain = rounded_parts(dve, (s_w, 10), w[0][:], w[1][:], w_raw)
            assert chain[1] == SETUP

            def taps_low(q, j, half):
                dve.wait_ge(s_th, 2 * q + half + 1)
                cols = slice(half * COLS, (half + 1) * COLS)
                dve.tensor_tensor(tp[half][64:STACK, :], raw[j % 2][64:STACK, cols],
                                  tp[half][64:STACK, :].bitcast(F32), ALU.subtract).then_inc(s_tl, 1)

            def spectrum_of(q, j, k):
                dve.wait_ge(s_f, KT * q + k + 1)
                dve.tensor_scalar(spectra[:, k, :, :, bass.ts(q, 2)].rearrange("p r w b -> p b w r"),
                                  f_banks[k][:, 0:2 * WINDOWS * ROWS].rearrange("p (b w r) -> p b w r", b=2, w=WINDOWS),
                                  1.0, None, ALU.mult).then_inc(s_e, 1)

            def step(q, j, t):
                dve.wait_ge(s_hh, q + 1)
                dve.scalar_tensor_tensor(hp[j % 2][1][:].rearrange("p b d -> p (b d)"), c_banks[j % 2][:], 0.0,
                                         hp[j % 2][0][:].rearrange("p b d -> p (b d)").bitcast(F32),
                                         ALU.max, ALU.subtract).then_inc(s_hl, 1)
                for k in range(KT):
                    if later(q, 1):
                        spectrum_of(q - 1, (j - 1) % 4, k)
                if not later(q, 1):
                    for half in range(2):
                        taps_low(q, j, half)
                if not isinstance(q, int) or q + 1 < PAIRS:
                    for half in range(2):
                        taps_low(q + 1, (j + 1) % 4, half)

            pairs(dve, step)
            for k in range(KT):
                spectrum_of(PAIRS - 1, 3, k)

        @block.tensor
        def _(pe):
            pe.wait_ge(s_diag, 4)
            for n in range(4):
                mm = nc.tensor.matmul(b_bank[:, n * P:(n + 1) * P], all_ones, diag[:, n * P:(n + 1) * P], start=True, stop=True)
            mm.then_inc(s_bc, 1)

            def conv1(q, j):
                i = j % 2
                pe.wait_ge(s_xl, q + 1)
                if later(q, 2):
                    pe.wait_ge(s_hl, q - 1)
                for b in range(2):
                    to = c_banks[i][:, b * D:(b + 1) * D]
                    n = 0
                    for l, r in ((0, 0), (0, 1), (1, 0)):
                        for k in range(KT):
                            nc.tensor.matmul(to, xp[i][l][:, k, b * P:(b + 1) * P], w[r][:, k, :], start=n == 0, stop=False)
                            n += 1
                    mm = nc.tensor.matmul(to, ones[:], bias[:], start=False, stop=True)
                mm.then_inc(s_c, 1)

            def dft_of(q, j):
                i = j % 2
                pe.wait_ge(s_hl, q + 1)
                size = WINDOWS * ROWS
                for k in range(KT):
                    if later(q, 1):
                        pe.wait_ge(s_e, KT * (q - 1) + k + 1)
                    for b in range(2):
                        for n, (l, r) in enumerate(((0, 0), (0, 1), (1, 0))):
                            mm = nc.tensor.matmul(f_banks[k][:, b * size:(b + 1) * size],
                                                  hp[i][l][:, b, k * P:(k + 1) * P], dft[r][:], start=n == 0, stop=n == 2)
                    mm.then_inc(s_f, 1)

            def taps_of(q):
                for half in range(2):
                    pe.wait_ge(s_tl, 2 * q + half + 1)
                    if later(q, 1):
                        pe.wait_ge(s_te, 2 * (q - 1) + half + 1)
                    nc.tensor.matmul(t_banks[half][0:ROWS, :], tdft[:], tp[half][:], start=True, stop=True).then_inc(s_tm, 1)

            pe.wait_ge(s_w, SETUP)
            conv1(0, 0)

            def step(q, j, t):
                if later(q, 1):
                    taps_of(q)
                if not isinstance(q, int) or q + 1 < PAIRS:
                    conv1(q + 1, (j + 1) % 4)
                dft_of(q, j)
                if not later(q, 1):
                    taps_of(q)

            pairs(pe, step)


def multiply_spectra(nc, spectra, weights_f, products_f):
    with ExitStack() as ctx:
        def sb(name, shape, dt=F32):
            return ctx.enter_context(nc.sbuf_tensor("ms_" + name, shape, dt))

        def sem(name):
            return ctx.enter_context(nc.semaphore("ms_" + name))

        w_raw = [sb(f"wf_raw_{i}", [P, KT, 2, D]) for i in range(2)]
        w = [[sb(f"wf_{part}_{i}", [P, KT, 2, D], F32R) for part in ("high", "low")] for i in range(2)]
        h = [[sb(f"hf_{part}_{i}", [P, KT, 2, P], F32R) for part in ("high", "low")] for i in range(WINDOWS)]
        b_copy = sb("b_copy", [P, 2, D])
        y = [sb(f"yf_{i}", [P, 2, D]) for i in range(WINDOWS)]
        a_banks = [ctx.enter_context(nc.psum_tensor(f"ms_a_{i}", [P, 2, D], F32)) for i in range(WINDOWS)]
        b_banks = [ctx.enter_context(nc.psum_tensor(f"ms_b_{i}", [P, 2, D], F32)) for i in range(WINDOWS)]

        s_in = [sem(f"wf_loaded_{i}") for i in range(2)]
        s_wh = sem("wf_high")
        s_wl = sem("wf_low")
        s_hh = sem("hf_high")
        s_hl = sem("hf_low")
        s_mm = sem("products_done")
        s_b = sem("b_copied")
        s_y = sem("y_done")
        s_st = [sem(f"y_stored_{i}") for i in range(WINDOWS)]
        block = ctx.enter_context(nc.Block())

        def frequencies(engine, step):
            for f in range(2):
                step(f, f, 0)
            with engine.Fori(1, FREQS // 2 - 1) as t:
                for i in range(2):
                    step(2 * t + i, i, t)
            for f in range(2 * (FREQS // 2 - 1), FREQS):
                step(f, f % 2, f // 2)

        @block.sync
        def _(sp):
            def load(f, i, t):
                if not (isinstance(f, int) and f < 2):
                    sp.wait_ge(s_wl, f - 1)
                for k in range(KT):
                    sp.dma_start(w_raw[i][:, k], weights_f[f, :, k].rearrange("r p o -> p r o")).then_inc(s_in[i], 16)

            load(0, 0, 0)
            load(1, 1, 0)

            def step(f, i, t):
                if not (isinstance(f, int) and f + 2 >= FREQS):
                    load(f + 2, i, t + 1)
                for v in range(WINDOWS):
                    sp.wait_ge(s_y, 2 * (WINDOWS * f + v + 1))
                    sp.dma_start(products_f[:, v, f], y[v][:]).then_inc(s_st[v], 16)

            frequencies(sp, step)
            for v in range(WINDOWS):
                sp.wait_ge(s_st[v], 16 * FREQS)

        @block.gpsimd
        def _(pool):
            def step(f, i, t):
                pool.wait_ge(s_wh, f + 1)
                pool.tensor_tensor(w[i][1][:], w_raw[i][:], w[i][0][:].bitcast(F32), ALU.subtract).then_inc(s_wl, 1)

            frequencies(pool, step)

        @block.scalar
        def _(act):
            def high(f, i, t):
                act.wait_ge(s_in[i], 32 * (t + 1))
                if not (isinstance(f, int) and f < 2):
                    act.wait_ge(s_mm, WINDOWS * (f - 1))
                act.activation(w[i][0][:], w_raw[i][:], ACT.Copy).then_inc(s_wh, 1)

            high(0, 0, 0)

            def step(f, i, t):
                if not (isinstance(f, int) and f + 1 >= FREQS):
                    high(f + 1, 1 - i, t + i)
                for v in range(WINDOWS):
                    act.wait_ge(s_mm, WINDOWS * f + v + 1)
                    wait(act, s_y, 2 * (WINDOWS * f + v))
                    parts = slice(1, 2) if isinstance(f, int) and f == 0 else slice(0, 2)
                    act.activation(b_copy[:, parts], b_banks[v][:, parts], ACT.Copy).then_inc(s_b, 1)

            frequencies(act, step)

        @block.vector
        def _(dve):
            def split(f, v, i):
                n = WINDOWS * f + v
                if not (isinstance(f, int) and f < 1):
                    dve.wait_ge(s_mm, n - WINDOWS + 1)
                source = spectra[:, :, bass.ts(f, 2), v, :]
                dve.tensor_scalar(h[v][0][:], source, 1.0, None, ALU.mult).then_inc(s_hh, 1)
                dve.wait_ge(s_hh, n + 1)
                dve.tensor_tensor(h[v][1][:], source, h[v][0][:].bitcast(F32), ALU.subtract).then_inc(s_hl, 1)

            for v in range(WINDOWS):
                split(0, v, 0)

            def step(f, i, t):
                for v in range(WINDOWS):
                    if not (isinstance(f, int) and f + 1 >= FREQS):
                        split(f + 1, v, 1 - i)
                    n = WINDOWS * f + v
                    dve.wait_ge(s_b, n + 1)
                    if not (isinstance(f, int) and f < 1):
                        dve.wait_ge(s_st[v], 16 * f)
                    if isinstance(f, int) and f == 0:
                        dve.tensor_copy(y[v][:, 0, :], a_banks[v][:, 0, :]).then_inc(s_y, 1)
                        dve.tensor_copy(y[v][:, 1, :], b_copy[:, 1, :]).then_inc(s_y, 1)
                    else:
                        dve.tensor_tensor(y[v][:, 0, :], a_banks[v][:, 0, :], b_copy[:, 1, :], ALU.subtract).then_inc(s_y, 1)
                        dve.tensor_tensor(y[v][:, 1, :], a_banks[v][:, 1, :], b_copy[:, 0, :], ALU.add).then_inc(s_y, 1)

            frequencies(dve, step)

        @block.tensor
        def _(pe):
            def step(f, i, t):
                pe.wait_ge(s_wl, f + 1)
                for v in range(WINDOWS):
                    pe.wait_ge(s_hl, WINDOWS * f + v + 1)
                    if not (isinstance(f, int) and f < 1):
                        pe.wait_ge(s_y, 2 * (WINDOWS * (f - 1) + v + 1))
                    for r, bank in ((0, a_banks[v]), (1, b_banks[v])):
                        parts = slice(r, r + 1) if isinstance(f, int) and f == 0 else slice(0, 2)
                        n = 0
                        for a, b in ((0, 0), (0, 1), (1, 0)):
                            for k in range(KT):
                                mm = nc.tensor.matmul(bank[:, parts], h[v][a][:, k, r, :], w[i][b][:, k, parts], start=n == 0, stop=n == 5)
                                n += 1
                    mm.then_inc(s_mm, 1)

            frequencies(pe, step)


def gated_layer_and_graph_layer(nc, xT, adjT, products_f, inverse_dft, bn2, w_seT, w_msgT, w_ihT, w_hhT, w_l1, se_bias,
                                msg_bias, gate_bias, l1_bias, identity, out):
    with ExitStack() as ctx:
        def sb(name, shape, dt=F32):
            return ctx.enter_context(nc.sbuf_tensor("gl_" + name, shape, dt))

        def sem(name):
            return ctx.enter_context(nc.semaphore("gl_" + name))

        def bank(name):
            return ctx.enter_context(nc.psum_tensor("gl_" + name, [P, COLS], F32))

        def pair(name, shape):
            return [sb(f"{name}_{part}", shape, F32R) for part in ("high", "low")]

        w_se = pair("w_se", [P, KT, SE_ROWS])
        w_msg = pair("w_msg", [P, KT, D])
        w_ih = pair("w_ih", [P, 2 * KT, 3 * D])
        w_hh = pair("w_hh", [P, KT, 3 * D])
        w_1 = pair("w_1", [P, KT, D])
        spectra_in = sb("spectra_in", [ROWS, 4 * WINDOWS, D])
        ident = sb("ident", [P, P])
        bse = sb("se_bias_rows", [P, 1])
        bmsg = sb("msg_bias", [P, D])
        inv_raw = sb("inverse_raw", [ROWS, WINDOWS, P])
        inv = pair("inverse", [ROWS, WINDOWS, P])
        bn_raw = sb("bn2_raw", [P, 4, KT])
        bl1 = sb("bl1", [P, D])
        bg_raw = sb("bg_raw", [P, 8, KT])
        bg = sb("bg", [P, 4, KT])
        minus_half = sb("minus_half", [P, GB])
        eps = sb("eps", [P, GB])
        mean_matrix = sb("mean_matrix", [P, P])
        carrier = sb("wait_carrier", [P, 1])

        x = [sb(f"x_{i}", [P, KT, COLS]) for i in range(2)]
        xp = [pair(f"x{i}", [P, KT, COLS]) for i in range(2)]
        yf = [spectra_in[:, 0:2 * WINDOWS], spectra_in[:, 2 * WINDOWS:]]
        yfp = pair("yf", [ROWS, 2 * WINDOWS, D])
        xc = sb("xc", [P, KT, COLS])
        xcp = [pair(f"xc{i}", [P, KT, COLS]) for i in range(2)]
        adj = sb("adj", [P, COLS])
        adj_o = sb("adj_o", [P, COLS])
        adjp = pair("adj", [P, COLS])
        se = sb("se", [P, COLS])
        left = sb("left", [P, COLS])
        right = sb("right", [P, COLS])
        e = sb("e", [P, COLS])
        a = sb("a", [P, COLS])
        a_parts = sb("a_parts", [P, 2, COLS], F32R)
        ap = [a_parts[:, part] for part in range(2)]
        msgp = pair("msg", [P, KT, COLS])
        nmpp = [pair(f"nmp{i}", [P, KT, COLS]) for i in range(2)]
        r = sb("r", [P, KT, COLS])
        z = sb("zg", [P, KT, COLS])
        n = sb("n", [P, KT, COLS])
        u = sb("u", [P, KT, COLS])
        stats = sb("stats", [P, 2, GB, 6])
        moments = sb("moments", [P, 2, GB, 2])
        rstd = sb("rstd", [P, 2, GB])
        x2 = sb("x2", [P, GB, D])
        x2b = sb("x2b", [P, GB, D])
        up = pair("u", [P, KT, COLS])
        supp = pair("sup", [P, GB, D])
        y = sb("y", [P, GB, D])
        res = sb("res", [P, GB, D])

        def flat(t):
            return t[:].rearrange("p a b -> p (a b)")[:, 0:3 * D]

        def tile_rows(src, k=None):
            return src.rearrange("(k p) m -> p k m", p=P) if k is None else src[k * P:(k + 1) * P, :]

        first_weights = [([p[:] for p in w_msg], res[:, 0:KT, :], tile_rows(w_msgT)),
                         ([p[:] for p in w_se], e[:, 0:KT * SE_ROWS].rearrange("p (k m) -> p k m", k=KT), tile_rows(w_seT))]
        gate_weights = [([p[:, k, :] for p in w_hh], flat(t), tile_rows(w_hhT, k)) for k, t in enumerate((x2, y))]
        gate_weights += [([p[:, k, :] for p in w_ih], flat(t), tile_rows(w_ihT, k)) for k, t in enumerate((r, z, n, u))]
        gate_weights += [([p[:] for p in w_1], res[:, KT:2 * KT, :], tile_rows(w_l1))]
        all_weights = first_weights + gate_weights

        gate_banks = [bank(f"gate_{i}") for i in range(3)]
        work = [bank(f"work_{i}") for i in range(5)]
        nmp_banks = [(work[3], work[4]), (work[2], gate_banks[1])]
        nmp = [e, a]
        msg_sum = [e, a]

        def nmp_sums(k, h):
            return nmp_banks[k][h][:].rearrange("p (b s n) -> p s b n", b=2, s=2)

        def nmp_of(k, h):
            return nmp[k][:, h * D:(h + 1) * D].rearrange("p (b n) -> p b n", b=2)

        s_load = [sem(f"weights_loaded_{j}") for j in range(len(all_weights))]
        s_wh = sem("weight_high")
        s_inv = sem("inverse_split")
        s_vec = sem("vectors_loaded")
        s_wl = sem("weight_low")
        s_mean = sem("w_1_mean")
        s_centred = sem("w_1_centred")
        s_init = sem("constants_ready")
        s_bg = sem("gate_bias_chain")
        s_x = [sem(f"x_loaded_{i}") for i in range(2)]
        s_yf = [sem(f"spectra_loaded_{j}") for j in range(2)]
        s_bn = sem("bn2_chain")
        s_adj = sem("adj_loaded")
        s_adjo = sem("adj_o_loaded")
        names = {}
        for name in ("x_high", "x_low", "yf_high", "yf_low", "xc_sum", "xc", "xc_high", "xc_low", "se", "left", "right", "e", "a", "a_high",
                     "a_low", "adj_high", "adj_low", "msg_sum", "msg_high", "msg_low", "nmp_part", "nmp_sum", "nmp_high", "nmp_low",
                     "r_tanh", "r_done", "z_tanh", "z_done", "rn", "n_in", "n_done", "diff", "zdiff", "nx",
                     "u_done", "stats", "moments", "var", "rstd", "x2", "x2b", "u_high", "u_low",
                     "sup_high", "sup_low", "y", "ystats", "ymoments", "yvar", "yrstd", "res",
                     "pe_se", "pe_msg", "pe_dist", "pe_nmp", "pe_r", "pe_hn", "pe_in", "pe_z",
                     "pe_yf", "conv_nodes", "pe_convT", "pe_uT", "pe_sup", "pe_out"):
            names[name] = sem("q_" + name)
        S = names
        s_out = sem("out_stored")
        block = ctx.enter_context(nc.Block())

        def steps(engine, step):
            def at(g, i):
                def has(k):
                    return 0 <= k < GROUPS
                step(g, i, g // 2, has(g), has(g + 1), has(g - 1), has(g - 2))

            for g in (-1, 0, 1):
                at(g, g % 2)
            with engine.Fori(1, GROUPS // 2 - 1) as t:
                for i in range(2):
                    step(2 * t + i, i, t, True, True, True, True)
            for g in range(GROUPS - 2, GROUPS + 2):
                at(g, g % 2)

        @block.sync
        def _(sp):
            def load_x(g, i):
                sp.dma_start(x[1 - i][:], xT[g + 1].rearrange("k p c -> p k c")).then_inc(s_x[1 - i], 16)

            load_x(-1, 1)
            for j, (_, stage, src) in enumerate(first_weights):
                sp.dma_start(stage, src).then_inc(s_load[j], 16)
            for dst, src in ((ident, identity), (bse, se_bias), (bmsg, msg_bias), (bl1, l1_bias),
                             (bg_raw, gate_bias), (inv_raw, inverse_dft), (bn_raw, bn2)):
                sp.dma_start(dst[:], src).then_inc(s_vec, 16)

            def step(g, i, t, now, ahead, behind, last):
                if ahead:
                    for j in range(2):
                        wait(sp, S["yf_low"], 2 * g + j + 1)
                        sp.dma_start(yf[j], products_f[bass.ts(2 * (g + 1) + j, 2)].rearrange("b w f r o -> (f r) (b w) o")).then_inc(s_yf[j], 16)
                    if now:
                        wait(sp, S["u_done"], KT * g)
                        load_x(g, i)
                    wait(sp, S["a"], g + 1)
                    sp.dma_start(adj[:], adjT[g + 1]).then_inc(s_adj, 16)
                if ahead and not now:
                    for j, (_, stage, src) in enumerate(gate_weights, len(first_weights)):
                        sp.dma_start(stage, src).then_inc(s_load[j], 16)
                if behind:
                    wait(sp, S["adj_low"], g - 1)
                    sp.dma_start(adj_o[:], adjT[g - 1]).then_inc(s_adjo, 16)
                if last:
                    sp.wait_ge(S["res"], GB * (g - 1))
                    sp.dma_start(out[bass.ts(g - 2, GB)].rearrange("b n d -> n b d"), res[:]).then_inc(s_out, 16)

            steps(sp, step)
            sp.wait_ge(s_out, 16 * GROUPS)

        @block.gpsimd
        def _(pool):
            pool.memset(left[:], 0.0).then_inc(s_init, 1)
            pool.memset(right[:], 0.0).then_inc(s_init, 1)
            pool.memset(minus_half[:], -0.5).then_inc(s_init, 1)
            pool.memset(eps[:], EPS).then_inc(s_init, 1)
            pool.memset(mean_matrix[:], 1.0 / D).then_inc(s_init, 1)
            pool.wait_ge(s_init, 5)
            pool.memset(left[64:64 + SE, :], -1.0).then_inc(s_init, 1)
            pool.wait_ge(s_init, 6)
            pool.memset(right[32:32 + SE, :], 1.0).then_inc(s_init, 1)
            pool.wait_ge(s_init, 7)

            def vectors():
                pool.wait_ge(s_vec, 16 * 7)
                chain = [(3, 3, eps[:, 0:KT], ALU.add), (3, 3, minus_half[:, 0:KT], ALU.pow), (0, 0, bn_raw[:, 3], ALU.mult),
                         (2, 2, bn_raw[:, 0], ALU.mult), (1, 1, bn_raw[:, 2], ALU.subtract)]
                for n_done, (to, of, other, op) in enumerate(chain):
                    pool.tensor_tensor(bn_raw[:, to], bn_raw[:, of], other, op).then_inc(s_bn, 1)
                    pool.wait_ge(s_bn, n_done + 1)
                pool.tensor_tensor(bg[:, 0:2, :], bg_raw[:, 0:2, :], bg_raw[:, 3:5, :], ALU.add).then_inc(s_bg, 1)
                pool.tensor_scalar(bg[:, 2, :], bg_raw[:, 2, :], 1.0, None, ALU.mult).then_inc(s_bg, 1)
                pool.tensor_scalar(bg[:, 3, :], bg_raw[:, 5, :], 1.0, None, ALU.mult).then_inc(s_bg, 1)
                pool.wait_ge(s_bg, 3)
                pool.tensor_scalar(bg[:, 0:2, :], bg[:, 0:2, :], 0.5, None, ALU.mult).then_inc(s_bg, 1)
                pool.wait_ge(s_bg, 4)

            def step(g, i, t, now, ahead, behind, last):
                if behind:
                    pool.wait_ge(S["moments"], GB * g)
                    pool.tensor_tensor(rstd[:, 0, :], moments[:, 0, :, 1], eps[:], ALU.add).then_inc(S["var"], 1)
                    pool.wait_ge(S["var"], g)
                    pool.tensor_tensor(rstd[:, 0, :], rstd[:, 0, :], minus_half[:], ALU.pow).then_inc(S["rstd"], 1)
                if ahead:
                    pool.wait_ge(S["x_high"], g + 2)
                    wait(pool, S["pe_z"], KT * g)
                    pool.tensor_tensor(xp[1 - i][1][:], x[1 - i][:], xp[1 - i][0][:].bitcast(F32), ALU.subtract).then_inc(S["x_low"], 1)
                if ahead and not now:
                    vectors()
                if last:
                    pool.wait_ge(S["ymoments"], GB * (g - 1))
                    pool.tensor_tensor(rstd[:, 1, :], moments[:, 1, :, 1], eps[:], ALU.add).then_inc(S["yvar"], 1)
                    pool.wait_ge(S["yvar"], g - 1)
                    pool.tensor_tensor(rstd[:, 1, :], rstd[:, 1, :], minus_half[:], ALU.pow).then_inc(S["yrstd"], 1)
                if behind:
                    pool.wait_ge(S["x2"], GB * g)
                    wait(pool, S["y"], 2 * (g - 1))
                    for b in range(GB):
                        pool.tensor_tensor(x2b[:, b, :], x2[:, b, :], bl1[:], ALU.add).then_inc(S["x2b"], 1)
                if ahead:
                    pool.wait_ge(S["se"], g + 2)
                    wait(pool, S["pe_dist"], g + 1)
                    pool.tensor_tensor(left[0:SE, :], se[0:SE, :], se[0:SE, :], ALU.add).then_inc(S["left"], 1)
                    pool.tensor_scalar(right[0:SE, :], se[0:SE, :], 1.0, None, ALU.mult).then_inc(S["right"], 1)
                    pool.wait_ge(S["right"], 2 * (g + 1) + 1)
                    pool.tensor_tensor(right[64:64 + SE, :], se[64:64 + SE, :], se[64:64 + SE, :], ALU.mult).then_inc(S["right"], 1)
                    pool.wait_ge(S["right"], 2 * (g + 2))
                if behind:
                    pool.wait_ge(S["adj_high"], g)
                    pool.tensor_tensor(adjp[1][:], adj_o[:], adjp[0][:].bitcast(F32), ALU.subtract).then_inc(S["adj_low"], 1)

                if ahead:
                    pool.wait_ge(S["xc_high"], g + 2)
                    pool.tensor_tensor(xcp[1 - i][1][:], xc[:], xcp[1 - i][0][:].bitcast(F32), ALU.subtract).then_inc(S["xc_low"], 1)

            steps(pool, step)

        @block.scalar
        def _(act):
            def weights_high(start, stop):
                for j in range(start, stop):
                    if j == len(all_weights) - 1:
                        act.wait_ge(s_centred, KT)
                    else:
                        act.wait_ge(s_load[j], 16)
                    act.activation(all_weights[j][0][0], all_weights[j][1], ACT.Copy).then_inc(s_wh, 1)

            weights_high(0, len(first_weights))

            def step(g, i, t, now, ahead, behind, last):
                def gate_tanh(k):
                    act.wait_ge(S["pe_r"], KT * g + k + 1)
                    if k == 0:
                        wait(act, S["n_done"], KT * g)
                    act.activation(r[:, k, :], gate_banks[k][:], ACT.Tanh, bias=bg[:, 0, k:k + 1], scale=0.5).then_inc(S["r_tanh"], 1)

                def spectra_high(j):
                    act.wait_ge(s_yf[j], 16 * (g + 2))
                    wait(act, S["pe_yf"], 2 * (g + 1) + j)
                    act.activation(yfp[0][:], yf[j], ACT.Copy).then_inc(S["yf_high"], 1)

                def conv_nodes(j):
                    act.wait_ge(S["pe_yf"], 2 * (g + 1) + j + 1)
                    act.activation(xc[:, j, :], work[j][:], ACT.Copy).then_inc(S["conv_nodes"], 1)

                def candidate(k):
                    act.wait_ge(S["n_in"], KT * g + k + 1)
                    if k == 0:
                        wait(act, S["nx"], KT * g)
                    act.activation(n[:, k, :], r[:, k, :], ACT.Tanh, bias=bg[:, 2, k:k + 1]).then_inc(S["n_done"], 1)

                def z_tanh(k):
                    act.wait_ge(S["pe_z"], KT * g + k + 1)
                    if k == 0:
                        wait(act, S["zdiff"], KT * g)
                    act.activation(z[:, k, :], gate_banks[0 if k == 0 else 2][:], ACT.Tanh, bias=bg[:, 1, k:k + 1], scale=0.5).then_inc(S["z_tanh"], 1)

                if now:
                    gate_tanh(0)
                if ahead:
                    act.wait_ge(s_x[1 - i], 16 * (t + 1 + i))
                    wait(act, S["pe_z"], KT * g)
                    act.activation(xp[1 - i][0][:], x[1 - i][:], ACT.Copy).then_inc(S["x_high"], 1)
                if behind:
                    act.wait_ge(S["u_done"], KT * g)
                    wait(act, S["pe_sup"], g - 1)
                    act.activation(up[0][:], u[:], ACT.Copy).then_inc(S["u_high"], 1)
                if now:
                    candidate(0)
                    z_tanh(0)
                if ahead:
                    spectra_high(0)
                if ahead:
                    if not now:
                        act.wait_ge(s_vec, 16 * 7)
                    act.wait_ge(S["pe_se"], g + 2)
                    wait(act, S["left"], 2 * (g + 1))
                    wait(act, S["right"], 2 * (g + 1))
                    act.activation(se[0:SE_ROWS, :], work[2][0:SE_ROWS, :], ACT.Identity, bias=bse[0:SE_ROWS, :]).then_inc(S["se"], 1)
                    for h in range(2):
                        act.wait_ge(S["msg_sum"], KT * (g + 1) + h + 1)
                        wait(act, S["pe_nmp"], KT * (g + 1))
                        act.activation(msgp[0][:, h, :], msg_sum[h][:], ACT.Relu).then_inc(S["msg_high"], 1)
                if now:
                    gate_tanh(1)
                if ahead:
                    wait(act, S["xc_low"], g + 1)
                    conv_nodes(0)
                    spectra_high(1)
                    act.wait_ge(S["pe_dist"], g + 2)
                    act.wait_ge(S["msg_low"], KT * (g + 2))
                    act.activation(e[:], work[2][:], ACT.Exp).then_inc(S["e"], 1)
                if ahead and not now:
                    weights_high(len(first_weights), len(all_weights))
                    act.wait_ge(s_bg, 4)
                    act.wait_ge(s_bn, 5)
                if behind:
                    act.wait_ge(s_adjo, 16 * g)
                    wait(act, S["pe_out"], g - 1)
                    act.activation(adjp[0][:], adj_o[:], ACT.Copy).then_inc(S["adj_high"], 1)
                    act.wait_ge(S["pe_sup"], g)
                    act.wait_ge(S["rstd"], g)
                    for b in range(GB):
                        act.activation(supp[0][:, b, :], work[3 + b // 2][:, (b % 2) * D:(b % 2 + 1) * D], ACT.Identity,
                                       scale=rstd[:, 0, b:b + 1]).then_inc(S["sup_high"], 1)
                if ahead:
                    conv_nodes(1)
                if now:
                    candidate(1)
                if ahead:
                    for k in range(KT):
                        act.wait_ge(S["xc_sum"], KT * (g + 1) + k + 1)
                        act.activation(xc[:, k, :], xc[:, k, :], ACT.Relu, bias=bn_raw[:, 1, k:k + 1]).then_inc(S["xc"], 1)
                    act.wait_ge(S["xc"], KT * (g + 2))
                    wait(act, S["pe_z"], KT * g)
                    act.activation(xcp[1 - i][0][:], xc[:], ACT.Copy).then_inc(S["xc_high"], 1)
                    for k in range(KT):
                        act.wait_ge(S["pe_nmp"], KT * (g + 1) + k + 1)
                        for h in range(2):
                            act.activation(nmp_of(k, h), nmp_sums(k, h)[:, 1], ACT.Copy).then_inc(S["nmp_part"], 1)
                    for k in range(KT):
                        act.wait_ge(S["nmp_sum"], GB * (g + 1) + 2 * (k + 1))
                        act.activation(nmpp[1 - i][0][:, k, :], nmp[k][:], ACT.Copy).then_inc(S["nmp_high"], 1)
                if now:
                    z_tanh(1)

            steps(act, step)

        @block.vector
        def _(dve):
            def weights_low(start, stop):
                for j in range(start, stop):
                    parts, stage, _ = all_weights[j]
                    dve.wait_ge(s_wh, j + 1)
                    dve.tensor_tensor(parts[1], stage, parts[0].bitcast(F32), ALU.subtract).then_inc(s_wl, 1)

            weights_low(0, len(first_weights))
            dve.wait_ge(s_vec, 16 * 7)
            rounded_parts(dve, (s_inv, 0), inv[0][:], inv[1][:], inv_raw[:])

            def step(g, i, t, now, ahead, behind, last):
                gate_hn = (1, 2)
                gate_in = (2, 0)

                def reset_and_sum(k):
                    dve.wait_ge(S["r_tanh"], KT * g + k + 1)
                    dve.tensor_scalar(r[:, k, :], r[:, k, :], 0.5, 0.5, ALU.mult, ALU.add).then_inc(S["r_done"], 1)
                    dve.wait_ge(S["r_done"], KT * g + k + 1)
                    dve.wait_ge(S["pe_hn"], KT * g + k + 1)
                    dve.scalar_tensor_tensor(r[:, k, :], gate_banks[gate_hn[k]][:], bg[:, 3, k:k + 1], r[:, k, :], ALU.add, ALU.mult).then_inc(S["rn"], 1)
                    dve.wait_ge(S["rn"], KT * g + k + 1)
                    dve.wait_ge(S["pe_in"], KT * g + k + 1)
                    dve.tensor_tensor(r[:, k, :], gate_banks[gate_in[k]][:], r[:, k, :], ALU.add).then_inc(S["n_in"], 1)

                def spectra_low(j):
                    dve.wait_ge(S["yf_high"], 2 * (g + 1) + j + 1)
                    dve.tensor_tensor(yfp[1][:], yf[j], yfp[0][:].bitcast(F32), ALU.subtract).then_inc(S["yf_low"], 1)

                def blend(k, group, i):
                    dve.wait_ge(S["n_done"], KT * group + k + 1)
                    if k == 0:
                        wait(dve, S["pe_uT"], group)
                        wait(dve, S["u_low"], group)
                    dve.tensor_tensor(u[:, k, :], x[i][:, k, :], n[:, k, :], ALU.subtract).then_inc(S["diff"], 1)
                    dve.tensor_tensor(n[:, k, :], x[i][:, k, :], n[:, k, :], ALU.add).then_inc(S["nx"], 1)
                    dve.wait_ge(S["z_tanh"], KT * group + k + 1)
                    dve.tensor_scalar(z[:, k, :], z[:, k, :], 0.5, 0.5, ALU.mult, ALU.add).then_inc(S["z_done"], 1)
                    dve.wait_ge(S["z_done"], KT * group + k + 1)
                    dve.wait_ge(S["diff"], KT * group + k + 1)
                    dve.tensor_tensor(u[:, k, :], z[:, k, :], u[:, k, :], ALU.mult).then_inc(S["zdiff"], 1)
                    dve.wait_ge(S["zdiff"], KT * group + k + 1)
                    dve.wait_ge(S["nx"], KT * group + k + 1)
                    dve.tensor_tensor(u[:, k, :], u[:, k, :], n[:, k, :], ALU.add).then_inc(S["u_done"], 1)

                def norm_stats(which, source, stats_sem, moments_sem, group):
                    for b in range(GB):
                        dve.bn_stats(stats[:, which, b, :], source(b)).then_inc(S[stats_sem], 1)
                    dve.wait_ge(S[stats_sem], GB * (group + 1))
                    dve.memset(carrier[:], 0.0)
                    for b in range(GB):
                        dve.bn_aggr(moments[:, which, b, :], stats[:, which, b, :]).then_inc(S[moments_sem], 1)

                if last:
                    dve.wait_ge(S["pe_out"], g - 1)
                    wait(dve, S["x2b"], GB * (g - 1))
                    wait(dve, S["res"], GB * (g - 2))
                    for h in range(2):
                        dve.tensor_tensor(y[:, 2 * h:2 * h + 2, :].rearrange("p b d -> p (b d)"), work[h][:],
                                          x2b[:, 2 * h:2 * h + 2, :].rearrange("p b d -> p (b d)"), ALU.add).then_inc(S["y"], 1)
                    dve.wait_ge(S["y"], 2 * (g - 1))
                    norm_stats(1, lambda b: y[:, b, :], "ystats", "ymoments", g - 2)
                if behind:
                    dve.wait_ge(S["pe_uT"], g)
                    norm_stats(0, lambda b: work[b // 2][:, (b % 2) * D:(b % 2 + 1) * D], "stats", "moments", g - 1)
                if now:
                    reset_and_sum(0)
                if behind:
                    dve.wait_ge(S["u_high"], g)
                    dve.tensor_tensor(up[1][:], u[:], up[0][:].bitcast(F32), ALU.subtract).then_inc(S["u_low"], 1)
                    dve.wait_ge(S["rstd"], g)
                    wait(dve, S["x2b"], GB * (g - 1))
                    for b in range(GB):
                        dve.tensor_scalar(x2[:, b, :], work[b // 2][:, (b % 2) * D:(b % 2 + 1) * D],
                                          moments[:, 0, b, 0:1], rstd[:, 0, b:b + 1], ALU.subtract, ALU.mult).then_inc(S["x2"], 1)
                if now:
                    blend(0, g, i)
                if ahead:
                    spectra_low(0)
                    dve.wait_ge(S["se"], g + 2)
                    wait(dve, S["pe_dist"], g + 1)
                    dve.scalar_tensor_tensor(left[32:32 + SE, :], se[32:32 + SE, :], -1.0, se[32:32 + SE, :], ALU.mult, ALU.mult).then_inc(S["left"], 1)
                    dve.wait_ge(S["pe_msg"], g + 2)
                    wait(dve, S["nmp_low"], KT * (g + 1))
                    for h in range(2):
                        dve.tensor_tensor(msg_sum[h][:].rearrange("p (b d) -> p b d", b=2), work[h][:].rearrange("p (b d) -> p b d", b=2),
                                          bmsg[:].unsqueeze(1).broadcast_to([P, 2, D]), ALU.add).then_inc(S["msg_sum"], 1)
                    for h in range(2):
                        dve.wait_ge(S["msg_high"], KT * (g + 1) + h + 1)
                        dve.scalar_tensor_tensor(msgp[1][:, h, :], msg_sum[h][:], 0.0, msgp[0][:, h, :].bitcast(F32), ALU.max, ALU.subtract).then_inc(S["msg_low"], 1)
                if last:
                    dve.wait_ge(S["yrstd"], g - 1)
                    wait(dve, s_out, 16 * (g - 2))
                    for b in range(GB):
                        dve.tensor_scalar(res[:, b, :], y[:, b, :], moments[:, 1, b, 0:1], rstd[:, 1, b:b + 1],
                                          ALU.subtract, ALU.mult).then_inc(S["res"], 1)
                if ahead:
                    spectra_low(1)
                    dve.wait_ge(S["msg_low"], KT * (g + 2))
                    dve.wait_ge(S["e"], g + 2)
                    dve.wait_ge(s_adj, 16 * (g + 2))
                    dve.tensor_tensor(a[:], e[:], adj[:], ALU.mult).then_inc(S["a"], 1)
                    dve.wait_ge(S["a"], g + 2)
                    dve.tensor_copy(ap[0], a[:]).then_inc(S["a_high"], 1)
                    dve.wait_ge(S["a_high"], g + 2)
                    dve.tensor_tensor(ap[1], a[:], ap[0].bitcast(F32), ALU.subtract).then_inc(S["a_low"], 1)
                if ahead and not now:
                    dve.wait_ge(s_mean, 1)
                    for k in range(KT):
                        dve.tensor_tensor(all_weights[-1][1][:, k], all_weights[-1][1][:, k], gate_banks[1][:, 0:D], ALU.subtract).then_inc(s_centred, 1)
                    weights_low(len(first_weights), len(all_weights))
                    dve.wait_ge(s_wl, len(all_weights))
                    dve.wait_ge(s_bn, 5)
                if behind:
                    for b in range(GB):
                        if b % 2 == 0:
                            dve.wait_ge(S["sup_high"], GB * (g - 1) + b + 2)
                        dve.scalar_tensor_tensor(supp[1][:, b, :], work[3 + b // 2][:, (b % 2) * D:(b % 2 + 1) * D],
                                                 rstd[:, 0, b:b + 1], supp[0][:, b, :].bitcast(F32),
                                                 ALU.mult, ALU.subtract).then_inc(S["sup_low"], 1)
                if now:
                    reset_and_sum(1)
                if ahead:
                    dve.wait_ge(S["pe_convT"], g + 2)
                    dve.wait_ge(S["x_high"], g + 2)
                    for k in range(KT):
                        dve.scalar_tensor_tensor(xc[:, k, :], work[k][:], bn_raw[:, 0, k:k + 1], x[1 - i][:, k, :], ALU.mult, ALU.add).then_inc(S["xc_sum"], 1)
                    for k in range(KT):
                        for h in range(2):
                            dve.wait_ge(S["nmp_part"], GB * (g + 1) + 2 * k + h + 1)
                            dve.tensor_tensor(nmp_of(k, h), nmp_sums(k, h)[:, 0], nmp_of(k, h), ALU.add).then_inc(S["nmp_sum"], 1)
                    for k in range(KT):
                        dve.wait_ge(S["nmp_high"], KT * (g + 1) + k + 1)
                        dve.tensor_tensor(nmpp[1 - i][1][:, k, :], nmp[k][:], nmpp[1 - i][0][:, k, :].bitcast(F32), ALU.subtract).then_inc(S["nmp_low"], 1)
                if now:
                    blend(1, g, i)

            steps(dve, step)

        @block.tensor
        def _(pe):
            pe.wait_ge(s_wl, len(first_weights))
            pe.wait_ge(s_init, 7)

            def products(out_, pairs):
                calls = [c for l, r_ in pairs for c in ((l[0], r_[0]), (l[0], r_[1]), (l[1], r_[0]))]
                for j, (l, r_) in enumerate(calls):
                    mm = nc.tensor.matmul(out_, l, r_, start=j == 0, stop=j == len(calls) - 1)
                return mm

            def step(g, i, t, now, ahead, behind, last):
                def weight(w, k, m):
                    return [p[:, k, m * P:(m + 1) * P] for p in w]

                def rows(pair_, k):
                    return [p[:, k, :] for p in pair_]

                def x_terms(m):
                    return [(weight(w_hh, k, m), rows(xp[i], k)) for k in range(KT)]

                def in_terms(m):
                    return ([(weight(w_ih, k, m), rows(xcp[i], k)) for k in range(KT)]
                            + [(weight(w_ih, KT + k, m), rows(nmpp[i], k)) for k in range(KT)])

                def gate_r(k):
                    if k == 0:
                        pe.wait_ge(S["xc_low"], g + 1)
                        pe.wait_ge(S["nmp_low"], KT * (g + 1))
                        wait(pe, S["n_in"], KT * g)
                    else:
                        pe.wait_ge(S["rn"], KT * g + 1)
                    products(gate_banks[k][:], x_terms(k) + in_terms(k)).then_inc(S["pe_r"], 1)

                def gate_hn(k):
                    if k == 1:
                        pe.wait_ge(S["n_in"], KT * g + 1)
                    else:
                        wait(pe, S["r_tanh"], KT * g)
                    products(gate_banks[1 + k][:], x_terms(2 * KT + k)).then_inc(S["pe_hn"], 1)

                def gate_in(k):
                    if k == 1:
                        pe.wait_ge(S["z_tanh"], KT * g + 1)
                    else:
                        wait(pe, S["z_tanh"], KT * g)
                    products(gate_banks[2 * (1 - k)][:], in_terms(2 * KT + k)).then_inc(S["pe_in"], 1)

                def gate_z(k):
                    if k == 0:
                        pe.wait_ge(S["r_tanh"], KT * g + 1)
                    else:
                        pe.wait_ge(S["rn"], KT * g + 2)
                    products(gate_banks[0 if k == 0 else 2][:], x_terms(KT + k) + in_terms(KT + k)).then_inc(S["pe_z"], 1)

                def transform_back(j):
                    if j == 0:
                        pe.wait_ge(S["msg_sum"], KT * (g + 2))
                    pe.wait_ge(S["yf_low"], 2 * (g + 1) + j + 1)
                    spectra = [p[:].rearrange("r (b w) o -> r w b o", w=WINDOWS) for p in yfp]
                    products(work[j][:].rearrange("p (b o) -> p b o", b=2),
                             [([p[:, v, :] for p in inv], [p[:, v] for p in spectra]) for v in range(WINDOWS)]).then_inc(S["pe_yf"], 1)

                if isinstance(g, int) and g == 0:
                    pe.wait_ge(s_wl, len(all_weights))
                if last:
                    pe.wait_ge(S["sup_low"], GB * (g - 1))
                    pe.wait_ge(S["adj_low"], g - 1)
                    wait(pe, S["xc_sum"], KT * (min(g + 1, GROUPS) if isinstance(g, int) else g + 1))
                    for b in range(GB):
                        cols = slice(b * P, (b + 1) * P)
                        mm = products(work[b // 2][:, (b % 2) * D:(b % 2 + 1) * D],
                                      [([p[:, cols] for p in adjp], [p[:, b, :] for p in supp])])
                    mm.then_inc(S["pe_out"], 1)
                if now:
                    gate_r(0)
                    gate_hn(0)
                if behind:
                    pe.wait_ge(S["u_done"], KT * g)
                    if last:
                        pe.wait_ge(S["y"], 2 * (g - 1))
                    elif now:
                        pe.wait_ge(S["xc_sum"], KT * (g + 1))
                    for b in range(GB):
                        for k in range(KT):
                            at = (b % 2) * D + k * P
                            mm = nc.tensor.transpose(work[b // 2][:, at:at + P], u[:, k, b * P:(b + 1) * P], ident[:])
                    mm.then_inc(S["pe_uT"], 1)
                if now:
                    gate_in(0)
                    gate_z(0)
                if ahead:
                    xn = xp[1 - i]
                    pe.wait_ge(S["x_low"], g + 2)
                    wait(pe, S["e"], g + 1)
                    products(work[2][0:SE_ROWS, :], [([p[:, k, :] for p in w_se], rows(xn, k)) for k in range(KT)]).then_inc(S["pe_se"], 1)
                    if not now:
                        pe.wait_ge(s_inv, 2)
                    if behind:
                        pe.wait_ge(S["x2"], GB * g)
                    else:
                        wait(pe, S["xc_sum"], KT * (g + 1))
                    for b in range(GB):
                        to = work[b // 2][:, (b % 2) * D:(b % 2 + 1) * D]
                        mm = products(to, [([p[:, k, b * P:(b + 1) * P] for p in xn], [p[:, k, :] for p in w_msg]) for k in range(KT)])
                    mm.then_inc(S["pe_msg"], 1)
                if now:
                    gate_r(1)
                if ahead:
                    transform_back(0)
                    pe.wait_ge(S["left"], 2 * (g + 2))
                    pe.wait_ge(S["right"], 2 * (g + 2))
                    for b in range(GB):
                        cols = slice(b * P, (b + 1) * P)
                        mm = nc.tensor.matmul(work[2][:, cols], left[0:SE_ROWS, cols], right[0:SE_ROWS, cols], start=True, stop=True)
                    mm.then_inc(S["pe_dist"], 1)
                if ahead and not now:
                    pe.wait_ge(s_load[-1], 16)
                    for k in range(KT):
                        mm = nc.tensor.matmul(gate_banks[1][:, 0:D], mean_matrix[:], all_weights[-1][1][:, k], start=k == 0, stop=k == KT - 1)
                    mm.then_inc(s_mean, 1)
                if behind:
                    pe.wait_ge(S["u_low"], g)
                    for b in range(GB):
                        mm = products(work[3 + b // 2][:, (b % 2) * D:(b % 2 + 1) * D],
                                      [([p[:, k, b * P:(b + 1) * P] for p in up], [p[:, k, :] for p in w_1]) for k in range(KT)])
                    mm.then_inc(S["pe_sup"], 1)
                if ahead:
                    transform_back(1)
                if now:
                    gate_hn(1)
                    gate_in(1)
                if ahead:
                    pe.wait_ge(S["conv_nodes"], 2 * (g + 2))
                    for k in range(KT):
                        for b in range(GB):
                            at = (b % 2) * D + k * P
                            mm = nc.tensor.transpose(work[k][:, b * P:(b + 1) * P], xc[:, b // 2, at:at + P], ident[:])
                    mm.then_inc(S["pe_convT"], 1)
                    pe.wait_ge(S["a_low"], g + 2)
                    pe.wait_ge(S["msg_low"], KT * (g + 2))
                    if behind:
                        pe.wait_ge(S["sup_low"], GB * g)
                    for k in range(KT):
                        for b in range(GB):
                            cols = slice(b * P, (b + 1) * P)
                            d0 = (b % 2) * D + k * P
                            to = nmp_banks[k][b // 2][:, (b % 2) * D:(b % 2 + 1) * D]
                            high, low = [p[:, b // 2, d0:d0 + P] for p in msgp]
                            nc.tensor.matmul(to.rearrange("p (s n) -> p s n", s=2), high, a_parts[:, :, cols], start=True, stop=False)
                            mm = nc.tensor.matmul(to[:, 0:P], low, ap[0][:, cols], start=False, stop=True)
                        mm.then_inc(S["pe_nmp"], 1)
                if now:
                    gate_z(1)

            steps(pe, step)


def _fourier_constants():
    import numpy as np

    def waves(at, sign):
        angle = 2 * np.pi * ((at[:, None] * np.arange(FREQS)) % WINDOW) / WINDOW
        both = np.stack([np.cos(angle), sign * np.sin(angle)], axis=2)
        both[:, 0, 1] = np.cos(np.pi * at)
        return both.reshape(len(at), ROWS)

    taps = waves(np.arange(TAPS), 1)
    bits = taps.astype(np.float32).view(np.uint32) & np.uint32(0xFFFFF000)
    high = bits.view(np.float32)
    tap_dft = np.zeros((STACK, ROWS), np.float32)
    tap_dft[0:TAPS] = high
    tap_dft[64:64 + TAPS] = high
    tap_dft[32:32 + TAPS] = taps - high
    row_dft = np.zeros((P, WINDOWS, ROWS))
    for w in range(WINDOWS):
        at = np.arange(P) - (w * OUTS - PAD)
        inside = (at >= 0) & (at < WINDOW)
        row_dft[inside, w] = waves(at[inside], -1)
    weight = np.full(ROWS, 2.0)
    weight[0:2] = 1.0
    inverse = np.zeros((ROWS, WINDOWS, P))
    for w in range(WINDOWS):
        inverse[:, w, w * OUTS:(w + 1) * OUTS] = waves(np.arange(OUTS), -1).T * weight[:, None] / WINDOW
    return {"tap_dft": tap_dft, "row_dft": row_dft.reshape(P, -1).astype(np.float32),
            "inverse_dft": inverse.astype(np.float32)}


def _layouts(inputs):
    import numpy as np

    c = {k: np.asarray(v) for k, v in inputs.items()}
    x, adj = c["x"], c["adj"]
    cols = lambda v: v.reshape(-1, P).T
    bn1 = [cols(c["L0_gnn_bn1_" + name]) for name in "gbmv"]
    taps = np.zeros((TAP_ROWS, D * D), c["L0_gnn_conv2_w"].dtype)
    taps[0:TAPS] = c["L0_gnn_conv2_w"].transpose(2, 1, 0).reshape(TAPS, D * D)
    bn2 = [cols(c["L0_gnn_bn2_" + name]) for name in "gbmv"]
    gates = [cols(c["L0_gnn_" + name][j * D:(j + 1) * D]) for name in ("b_ih", "b_hh") for j in range(3)]
    gates += [np.zeros_like(gates[0])] * 2
    w_se, b_se = c["L0_gnn_w_se"], c["L0_gnn_b_se"]
    w_seT = np.zeros((D, SE_ROWS), w_se.dtype)
    se_bias = np.zeros((P, 1), b_se.dtype)
    for q in range(3):
        w_seT[:, 32 * q:32 * q + SE] = w_se.T
        se_bias[32 * q:32 * q + SE, 0] = b_se
    return {
        "xT": x.reshape(GROUPS, GB, P, KT, P).transpose(0, 3, 4, 1, 2).reshape(GROUPS, KT, P, COLS),
        "adjT": adj.reshape(GROUPS, GB, P, P).transpose(0, 3, 1, 2).reshape(GROUPS, P, COLS),
        "conv1_wT": c["L0_gnn_conv1_w"][:, :, 0].T.reshape(KT, P, D).transpose(1, 0, 2),
        "taps": taps,
        "bn1": np.stack(bn1, axis=1),
        "bn2": np.stack(bn2, axis=1),
        "w_seT": w_seT,
        "w_msgT": c["L0_gnn_w_msg"].T,
        "w_ihT": c["L0_gnn_w_ih"].T,
        "w_hhT": c["L0_gnn_w_hh"].T,
        "w_l1": c["L1_gnn_weight"],
        "se_bias": se_bias,
        "msg_bias": np.broadcast_to(c["L0_gnn_b_msg"], (P, D)),
        "gate_bias": np.stack(gates, axis=1),
        "l1_bias": np.broadcast_to(c["L1_gnn_bias"], (P, D)),
        "identity": np.eye(P, dtype=np.float32),
        **_fourier_constants(),
    }


def kernel(**inputs):
    import numpy as np
    import concourse.bacc as bacc
    from concourse.bass_utils import run_bass_kernel_spmd

    nc = bacc.Bacc("TRN2", target_bir_lowering=False, num_devices=1)
    arrays = {name: np.ascontiguousarray(a) for name, a in _layouts(inputs).items()}
    t = {name: nc.dram_tensor(name, a.shape, mybir.dt.from_np(a.dtype), kind="ExternalInput").ap()
         for name, a in arrays.items()}
    out = nc.dram_tensor("out", (GROUPS * GB, P, D), F32, kind="ExternalOutput").ap()
    weights_f = nc.dram_tensor("weights_f", (ROWS, D * D), F32, kind="Internal").ap()
    products_f = nc.dram_tensor("products_f", (GROUPS * GB, WINDOWS, FREQS, 2, D), F32, kind="Internal").ap()
    with nc.sbuf_tensor("spectra", [P, KT, ROWS, WINDOWS, P], F32) as spectra:
        transform_weights_and_rows(nc, t["taps"], t["tap_dft"], t["xT"], t["conv1_wT"], t["bn1"], t["identity"],
                                   t["row_dft"], weights_f, spectra)
        multiply_spectra(nc, spectra, weights_f.rearrange("(f r) (k p o) -> f r k p o", r=2, k=KT, p=P), products_f)
    gated_layer_and_graph_layer(nc, t["xT"], t["adjT"], products_f, t["inverse_dft"], t["bn2"], t["w_seT"],
                                t["w_msgT"], t["w_ihT"], t["w_hhT"], t["w_l1"], t["se_bias"], t["msg_bias"],
                                t["gate_bias"], t["l1_bias"], t["identity"], out)
    r = run_bass_kernel_spmd(nc, [arrays], core_ids=[0])
    return r.results[0]["out"]
```
